# Optimizing a Trainium2 kernel written in Bass

```python
import numpy as np
import jax
import jax.numpy as jnp

def _softmax(x, axis=-1):
    return jax.nn.softmax(x, axis=axis)

def _gelu(x):
    return jax.nn.gelu(x, approximate=True)

def _silu(x):
    return jax.nn.silu(x)

def _sigmoid(x):
    return jax.nn.sigmoid(x)

def _layernorm(x, axis=-1, eps=1e-05):
    m = jnp.mean(x, axis=axis, keepdims=True)
    v = jnp.var(x, axis=axis, keepdims=True)
    return (x - m) / jnp.sqrt(v + eps)

def _scatter_add(tgt, idx, src, axis=0):
    return tgt.at[idx].add(src)

def _segment_sum(src, seg, n):
    return jax.ops.segment_sum(src, seg, n)
kernel_name = 'mk_macaron_d2_jaxref_r8_e890ac'

def setup_inputs(seed: int=0):
    np.random.seed(seed)
    _w = jnp.asarray

    def _L0_attn_setup():
        import math
        import jax, jax.numpy as jnp
        import numpy as np
        C = 8.0
        _MIN_RAD, _MAX_RAD = (0.9, 0.999)

        def block_diag_linear(x, w):
            B, T, D = x.shape
            H, bs, _ = w.shape
            xh = x.reshape(B, T, H, bs)
            return jnp.einsum('bthd,hde->bthe', xh, w).reshape(B, T, D)

        def linear_scan(a, b):

            def op(l, r):
                a1, b1 = l
                a2, b2 = r
                return (a1 * a2, a2 * b1 + b2)
            return jax.lax.associative_scan(op, (a, b), axis=1)[1]

        def _reference_tuple_inner(x, a_param, w_in, w_a):
            gate_x = jax.nn.sigmoid(block_diag_linear(x, w_in))
            gate_a = jax.nn.sigmoid(block_diag_linear(x, w_a))
            log_a = -C * jax.nn.softplus(a_param) * gate_a
            a = jnp.exp(log_a)
            multiplier = jnp.sqrt(1.0 - jnp.exp(2.0 * log_a))
            b = multiplier * (gate_x * x)
            y = linear_scan(a, b)
            h_last = y[:, -1, :]
            return (y, h_last)
        key = jax.random.key(seed)
        k1, k2, k3, k4 = jax.random.split(key, 4)
        B, T, D, H = (4, 512, 128, 8)
        bs = D // H
        x = jax.random.normal(k1, (B, T, D), dtype=jnp.float32)
        std = 1.0 / math.sqrt(bs)
        w_in = jax.random.normal(k2, (H, bs, bs), dtype=jnp.float32) * std
        w_a = jax.random.normal(k3, (H, bs, bs), dtype=jnp.float32) * std
        sp = jax.random.uniform(k4, (D,), dtype=jnp.float32, minval=-math.log(_MAX_RAD) / C, maxval=-math.log(_MIN_RAD) / C)
        a_param = jnp.log(jnp.exp(sp) - 1.0 + 1e-08)
        return {'x': x, 'a_param': a_param, 'w_in': w_in, 'w_a': w_a}
    _L0_attn_in = _L0_attn_setup()

    def _L0_ffn_setup():
        import jax, jax.numpy as jnp
        import numpy as np
        LN_EPS = 1e-05

        def entmax15(z):
            z = z / 2.0
            z = z - jnp.max(z, axis=-1, keepdims=True)
            zs = -jnp.sort(-z, axis=-1)
            k = jnp.arange(1, z.shape[-1] + 1, dtype=z.dtype)
            mean = jnp.cumsum(zs, axis=-1) / k
            meansq = jnp.cumsum(zs * zs, axis=-1) / k
            ss = k * (meansq - jnp.square(mean))
            delta = (1.0 - ss) / k
            tau = mean - jnp.sqrt(jnp.clip(delta, 0.0))
            support = jnp.sum((tau <= zs).astype(jnp.int32), axis=-1, keepdims=True)
            tau_star = jnp.take_along_axis(tau, support - 1, axis=-1)
            return jnp.square(jnp.clip(z - tau_star, 0.0))

        def layernorm_noaffine(v):
            m = jnp.mean(v, axis=-1, keepdims=True)
            var = jnp.mean(jnp.square(v - m), axis=-1, keepdims=True)
            return (v - m) / jnp.sqrt(var + LN_EPS)

        def cp_mumoe(x, gate, Win, Wout):
            ones = jnp.ones(x.shape[:-1] + (1,), x.dtype)
            xb = jnp.concatenate([x, ones], axis=-1)
            z = jnp.einsum('btd,dr->btr', xb, Win) * gate
            return jnp.einsum('btr,or->bto', z, Wout)
        key = jax.random.key(seed)
        ks = jax.random.split(key, 8)
        B, T, D, O, D2, E, R = (8, 256, 128, 512, 128, 16, 64)
        s = lambda k, shape, scale: jax.random.normal(k, shape, jnp.float32) * scale
        return {'x': s(ks[0], (B, T, D), 1.0), 'proj': s(ks[1], (D, E), D ** (-0.5)), 'C1': s(ks[2], (E, R), E ** (-0.5)), 'Win1': s(ks[3], (D + 1, R), D ** (-0.5)), 'Wout1': s(ks[4], (O, R), R ** (-0.5)), 'C2': s(ks[5], (E, R), E ** (-0.5)), 'Win2': s(ks[6], (O + 1, R), O ** (-0.5)), 'Wout2': s(ks[7], (D2, R), R ** (-0.5))}
    _L0_ffn_in = _L0_ffn_setup()

    def _L1_attn_setup():
        import jax, jax.numpy as jnp
        import numpy as np
        NUM_HEADS = 16
        key = jax.random.key(seed)
        k1, k2, k3 = jax.random.split(key, 3)
        T, B, D = (256, 4, 128)
        x = jax.random.normal(k1, (T, B, D), dtype=jnp.float32)
        limit = float(np.sqrt(6.0 / (3 * D + D)))
        in_proj_weight = jax.random.uniform(k2, (3 * D, D), dtype=jnp.float32, minval=-limit, maxval=limit)
        in_proj_bias = jnp.zeros((3 * D,), dtype=jnp.float32)
        lim2 = float(np.sqrt(1.0 / D))
        out_w = jax.random.uniform(k3, (D, D), dtype=jnp.float32, minval=-lim2, maxval=lim2)
        out_b = jnp.zeros((D,), dtype=jnp.float32)
        return {'x': x, 'in_proj_weight': in_proj_weight, 'in_proj_bias': in_proj_bias, 'out_w': out_w, 'out_b': out_b}
    _L1_attn_in = _L1_attn_setup()

    def _L1_ffn_setup():
        import jax, jax.numpy as jnp
        import numpy as np
        HIDDEN = 128
        HEAD_DIM = 64
        N_EXPERTS = 16
        MIN_EXPERTS = 2
        B, T = (4, 256)

        def _normalize(x, axis):
            n = jnp.sqrt(jnp.sum(x * x, axis=axis, keepdims=True))
            return x / jnp.maximum(n, 1e-12)

        def _ste(x):
            hard = jax.lax.stop_gradient((x > 0).astype(x.dtype))
            return hard + x - jax.lax.stop_gradient(x)

        def _gating(hidden_states, sim_matrix, gates):
            b, t, c = hidden_states.shape
            flat = hidden_states.reshape(b * t, c)
            logits = _normalize(flat, -1) @ _normalize(sim_matrix, 0) - jax.nn.sigmoid(gates)
            gated = jax.nn.relu(logits)
            mask = _ste(gated)
            inactive = jnp.sum(mask, axis=1) == 0
            _, fb_idx = jax.lax.top_k(logits, MIN_EXPERTS)
            fb = jnp.zeros_like(mask).at[jnp.arange(b * t)[:, None], fb_idx].set(1.0)
            fb_applied = inactive[:, None] & (fb > 0)
            mask = jnp.where(fb_applied, 1.0, mask)
            masked_logits = jnp.where(mask > 0, gated, -jnp.inf)
            return jax.nn.softmax(masked_logits, axis=-1).reshape(b, t, -1)
        key = jax.random.key(seed)
        ks = jax.random.split(key, 6)
        xav_qkv = float(np.sqrt(6.0 / (HIDDEN + HEAD_DIM)))
        return {'hidden_states': jax.random.normal(ks[0], (B, T, HIDDEN), dtype=jnp.float32), 'sim_matrix': jax.random.normal(ks[1], (HIDDEN, N_EXPERTS), dtype=jnp.float32), 'gates': jnp.zeros((N_EXPERTS,), dtype=jnp.float32), 'q_proj': jax.random.uniform(ks[2], (N_EXPERTS, HIDDEN, HEAD_DIM), jnp.float32, -xav_qkv, xav_qkv), 'k_proj': jax.random.uniform(ks[3], (N_EXPERTS, HIDDEN, HEAD_DIM), jnp.float32, -xav_qkv, xav_qkv), 'v_proj': jax.random.uniform(ks[4], (N_EXPERTS, HIDDEN, HEAD_DIM), jnp.float32, -xav_qkv, xav_qkv), 'o_proj': jax.random.uniform(ks[5], (N_EXPERTS, HEAD_DIM, HIDDEN), jnp.float32, -xav_qkv, xav_qkv)}
    _L1_ffn_in = _L1_ffn_setup()
    _d = {'L0_attn_x': _L0_attn_in['x'], 'L0_attn_a_param': _L0_attn_in['a_param'], 'L0_attn_w_in': _L0_attn_in['w_in'], 'L0_attn_w_a': _L0_attn_in['w_a'], 'L0_ffn_proj': _L0_ffn_in['proj'], 'L0_ffn_C1': _L0_ffn_in['C1'], 'L0_ffn_Win1': _L0_ffn_in['Win1'], 'L0_ffn_Wout1': _L0_ffn_in['Wout1'], 'L0_ffn_C2': _L0_ffn_in['C2'], 'L0_ffn_Win2': _L0_ffn_in['Win2'], 'L0_ffn_Wout2': _L0_ffn_in['Wout2'], 'L1_attn_in_proj_weight': _L1_attn_in['in_proj_weight'], 'L1_attn_in_proj_bias': _L1_attn_in['in_proj_bias'], 'L1_attn_out_w': _L1_attn_in['out_w'], 'L1_attn_out_b': _L1_attn_in['out_b'], 'L1_ffn_sim_matrix': _L1_ffn_in['sim_matrix'], 'L1_ffn_gates': _L1_ffn_in['gates'], 'L1_ffn_q_proj': _L1_ffn_in['q_proj'], 'L1_ffn_k_proj': _L1_ffn_in['k_proj'], 'L1_ffn_v_proj': _L1_ffn_in['v_proj'], 'L1_ffn_o_proj': _L1_ffn_in['o_proj']}
    _x0 = _d['L0_attn_x']
    _d['L0_attn_x'] = jax.random.normal(jax.random.fold_in(jax.random.key(seed), 1), (2, 2048, 128), dtype=_x0.dtype)
    del _x0
    return _d

def reference(L0_attn_x, L0_attn_a_param, L0_attn_w_in, L0_attn_w_a, L0_ffn_proj, L0_ffn_C1, L0_ffn_Win1, L0_ffn_Wout1, L0_ffn_C2, L0_ffn_Win2, L0_ffn_Wout2, L1_attn_in_proj_weight, L1_attn_in_proj_bias, L1_attn_out_w, L1_attn_out_b, L1_ffn_sim_matrix, L1_ffn_gates, L1_ffn_q_proj, L1_ffn_k_proj, L1_ffn_v_proj, L1_ffn_o_proj):

    def _L0_attn_ref(x, a_param, w_in, w_a):
        import math
        import jax, jax.numpy as jnp
        import numpy as np
        C = 8.0
        _MIN_RAD, _MAX_RAD = (0.9, 0.999)

        def block_diag_linear(x, w):
            B, T, D = x.shape
            H, bs, _ = w.shape
            xh = x.reshape(B, T, H, bs)
            return jnp.einsum('bthd,hde->bthe', xh, w).reshape(B, T, D)

        def linear_scan(a, b):

            def op(l, r):
                a1, b1 = l
                a2, b2 = r
                return (a1 * a2, a2 * b1 + b2)
            return jax.lax.associative_scan(op, (a, b), axis=1)[1]

        def _reference_tuple_inner(x, a_param, w_in, w_a):
            gate_x = jax.nn.sigmoid(block_diag_linear(x, w_in))
            gate_a = jax.nn.sigmoid(block_diag_linear(x, w_a))
            log_a = -C * jax.nn.softplus(a_param) * gate_a
            a = jnp.exp(log_a)
            multiplier = jnp.sqrt(1.0 - jnp.exp(2.0 * log_a))
            b = multiplier * (gate_x * x)
            y = linear_scan(a, b)
            h_last = y[:, -1, :]
            return (y, h_last)
        return _reference_tuple_inner(x, a_param, w_in, w_a)[0]

    def _L0_ffn_ref(x, proj, C1, Win1, Wout1, C2, Win2, Wout2):
        import jax, jax.numpy as jnp
        import numpy as np
        LN_EPS = 1e-05

        def entmax15(z):
            z = z / 2.0
            z = z - jnp.max(z, axis=-1, keepdims=True)
            zs = -jnp.sort(-z, axis=-1)
            k = jnp.arange(1, z.shape[-1] + 1, dtype=z.dtype)
            mean = jnp.cumsum(zs, axis=-1) / k
            meansq = jnp.cumsum(zs * zs, axis=-1) / k
            ss = k * (meansq - jnp.square(mean))
            delta = (1.0 - ss) / k
            tau = mean - jnp.sqrt(jnp.clip(delta, 0.0))
            support = jnp.sum((tau <= zs).astype(jnp.int32), axis=-1, keepdims=True)
            tau_star = jnp.take_along_axis(tau, support - 1, axis=-1)
            return jnp.square(jnp.clip(z - tau_star, 0.0))

        def layernorm_noaffine(v):
            m = jnp.mean(v, axis=-1, keepdims=True)
            var = jnp.mean(jnp.square(v - m), axis=-1, keepdims=True)
            return (v - m) / jnp.sqrt(var + LN_EPS)

        def cp_mumoe(x, gate, Win, Wout):
            ones = jnp.ones(x.shape[:-1] + (1,), x.dtype)
            xb = jnp.concatenate([x, ones], axis=-1)
            z = jnp.einsum('btd,dr->btr', xb, Win) * gate
            return jnp.einsum('btr,or->bto', z, Wout)
        a = entmax15(layernorm_noaffine(jnp.einsum('btd,de->bte', x, proj)))
        g1 = jnp.einsum('bte,er->btr', a, C1)
        h = cp_mumoe(x, g1, Win1, Wout1)
        h = jax.nn.gelu(h, approximate=False)
        g2 = jnp.einsum('bte,er->btr', a, C2)
        return cp_mumoe(h, g2, Win2, Wout2)

    def _L1_attn_ref(x, in_proj_weight, in_proj_bias, out_w, out_b):
        import jax, jax.numpy as jnp
        import numpy as np
        NUM_HEADS = 16
        T, B, D = x.shape
        H = NUM_HEADS
        hd = D // H
        scaling = hd ** (-0.5)
        qkv = jnp.einsum('tbd,ed->tbe', x, in_proj_weight) + in_proj_bias
        q, k, v = jnp.split(qkv, 3, axis=-1)
        q = q * scaling

        def to_heads(t):
            return t.reshape(T, B * H, hd).transpose(1, 0, 2)
        q, k, v = (to_heads(q), to_heads(k), to_heads(v))
        scores = jnp.einsum('nqd,nkd->nqk', q, k)
        attn = jax.nn.softmax(scores, axis=-1)
        out = jnp.einsum('nqk,nkd->nqd', attn, v)
        out = out.transpose(1, 0, 2).reshape(T, B, D)
        return jnp.einsum('tbd,ed->tbe', out, out_w) + out_b

    def _L1_ffn_ref(hidden_states, sim_matrix, gates, q_proj, k_proj, v_proj, o_proj):
        import jax, jax.numpy as jnp
        import numpy as np
        HIDDEN = 128
        HEAD_DIM = 64
        N_EXPERTS = 16
        MIN_EXPERTS = 2
        B, T = (4, 256)

        def _normalize(x, axis):
            n = jnp.sqrt(jnp.sum(x * x, axis=axis, keepdims=True))
            return x / jnp.maximum(n, 1e-12)

        def _ste(x):
            hard = jax.lax.stop_gradient((x > 0).astype(x.dtype))
            return hard + x - jax.lax.stop_gradient(x)

        def _gating(hidden_states, sim_matrix, gates):
            b, t, c = hidden_states.shape
            flat = hidden_states.reshape(b * t, c)
            logits = _normalize(flat, -1) @ _normalize(sim_matrix, 0) - jax.nn.sigmoid(gates)
            gated = jax.nn.relu(logits)
            mask = _ste(gated)
            inactive = jnp.sum(mask, axis=1) == 0
            _, fb_idx = jax.lax.top_k(logits, MIN_EXPERTS)
            fb = jnp.zeros_like(mask).at[jnp.arange(b * t)[:, None], fb_idx].set(1.0)
            fb_applied = inactive[:, None] & (fb > 0)
            mask = jnp.where(fb_applied, 1.0, mask)
            masked_logits = jnp.where(mask > 0, gated, -jnp.inf)
            return jax.nn.softmax(masked_logits, axis=-1).reshape(b, t, -1)
        b, t, c = hidden_states.shape
        rw = _gating(hidden_states, sim_matrix, gates)
        q = jnp.einsum('bte,bted->btd', rw, jnp.einsum('btc,ecd->bted', hidden_states, q_proj))
        k = jnp.einsum('bte,bted->btd', rw, jnp.einsum('btc,ecd->bted', hidden_states, k_proj))
        v = jnp.einsum('bte,bted->btd', rw, jnp.einsum('btc,ecd->bted', hidden_states, v_proj))
        scale = 1.0 / jnp.sqrt(jnp.asarray(HEAD_DIM, dtype=q.dtype))
        scores = jnp.einsum('bqd,bkd->bqk', q, k) * scale
        causal = jnp.tril(jnp.ones((t, t), dtype=bool))
        scores = jnp.where(causal, scores, -jnp.inf)
        attn = jnp.einsum('bqk,bkd->bqd', jax.nn.softmax(scores, axis=-1), v)
        mixed = attn[:, :, None, :] * rw[..., None]
        return jnp.einsum('bted,edc->btc', mixed, o_proj)
    x = L0_attn_x
    x = x + 0.5 * _L0_ffn_ref(_layernorm(x, axis=-1), L0_ffn_proj, L0_ffn_C1, L0_ffn_Win1, L0_ffn_Wout1, L0_ffn_C2, L0_ffn_Win2, L0_ffn_Wout2)
    x = x + _L0_attn_ref(_layernorm(x, axis=-1), L0_attn_a_param, L0_attn_w_in, L0_attn_w_a)
    x = x + 0.5 * _L0_ffn_ref(_layernorm(x, axis=-1), L0_ffn_proj, L0_ffn_C1, L0_ffn_Win1, L0_ffn_Wout1, L0_ffn_C2, L0_ffn_Win2, L0_ffn_Wout2)
    x = x + 0.5 * _L1_ffn_ref(_layernorm(x, axis=-1), L1_ffn_sim_matrix, L1_ffn_gates, L1_ffn_q_proj, L1_ffn_k_proj, L1_ffn_v_proj, L1_ffn_o_proj)
    x = x + _L1_attn_ref(_layernorm(x, axis=-1), L1_attn_in_proj_weight, L1_attn_in_proj_bias, L1_attn_out_w, L1_attn_out_b)
    x = x + 0.5 * _L1_ffn_ref(_layernorm(x, axis=-1), L1_ffn_sim_matrix, L1_ffn_gates, L1_ffn_q_proj, L1_ffn_k_proj, L1_ffn_v_proj, L1_ffn_o_proj)
    return x

_drawn_inputs = setup_inputs


def setup_inputs(seed=0):
    import zlib

    import numpy as np

    out = dict(_drawn_inputs(seed))
    spreads = {'L1_attn_in_proj_bias': (0.0, 0.8),
     'L1_attn_out_b': (0.0, 0.8),
     'L1_ffn_gates': (0.0, 0.8)}
    factors = {'L0_ffn_proj': 4.28,
     'L0_ffn_C1': 4.396,
     'L0_ffn_Win1': 4.223,
     'L0_ffn_Wout1': 4.423,
     'L0_ffn_C2': 3.657,
     'L0_ffn_Win2': 3.647,
     'L0_ffn_Wout2': 3.624,
     'L1_ffn_q_proj': 29.024,
     'L1_ffn_k_proj': 28.104,
     'L0_attn_w_a': 2.798,
     'L1_attn_in_proj_weight': 8.0,
     'L1_attn_out_w': 8.0,
     'L1_ffn_sim_matrix': 8.0,
     'L1_ffn_v_proj': 8.0,
     'L1_ffn_o_proj': 8.0}
    for name, (base, spread) in spreads.items():
        noise = np.random.default_rng([zlib.crc32(name.encode()), seed]).standard_normal(out[name].shape)
        drawn = base * np.exp(spread * noise) if base else spread * noise
        out[name] = jnp.asarray(drawn.astype(out[name].dtype))
    for name, factor in factors.items():
        out[name] = (out[name] * factor).astype(out[name].dtype)
    return out
```

```python
from contextlib import ExitStack, contextmanager

import numpy as np

import concourse.bass as bass
from concourse import mybir

STAGES = 6

B, T, D = 2, 2048, 128
P = 128
TILES = B * T // P
ROW_TILES = T // P
CT = 4
CHUNK = CT * P
CHUNKS = TILES // CT
E, R, O = 16, 64, 512
OC = O // P
BANK = 512
LN_EPS = 1e-5
LRU_C = 8.0
LRU_HEADS = 8
HD = 64
QKV = 3 * HD
HEADS = 16
GROUPS = sum(i // CT + 1 for i in range(ROW_TILES))
HEAD = 2
RING = 4

KIND = ("ffn", "lru", "ffn", "moe", "mha", "moe")
REP = (0, 0, 1, 0, 0, 1)
FIRSTS = (0, 1, 3, 4)

F32 = mybir.dt.float32
ALU = mybir.AluOpType
ACT = mybir.ActivationFunctionType
AX = mybir.AxisListType


def after(c):
    return c + (1 + HEAD)


def free(c):
    return c + (1 + HEAD - 2)


def counted(s):
    return REP[s] * CHUNKS, REP[s] * TILES, REP[s] * B * GROUPS


class Steps:

    def __init__(self, engine, semaphore):
        self.engine, self.semaphore, self.base, self.n = engine, semaphore, 0, 0

    def did(self, instruction):
        instruction.then_inc(self.semaphore, 1)
        self.n += 1

    def settle(self):
        self.engine.wait_ge(self.semaphore, self.base + self.n)

    @contextmanager
    def loop(self, start, end, per):
        outer = self.base + self.n
        with self.engine.Fori(start, end) as i:
            self.base, self.n = (i - start) * per + outer, 0
            yield i
            assert self.n == per, f"{self.n} steps in a body of {per}"
        self.base, self.n = outer + (end - start) * per, 0


def program(nc, x_in, out, w):
    ctx = ExitStack()
    with ctx:
        def sb(name, shape):
            return ctx.enter_context(nc.sbuf_tensor(name, shape, F32))

        sems = {}

        def sem(name, stage=None):
            name = name if stage is None else f"{KIND[stage]}_{name}"
            if name not in sems:
                sems[name] = ctx.enter_context(nc.semaphore(name))
            return sems[name]

        X = sb("X", [P, TILES, D])
        X_rows = X[:, :, :].rearrange("p (b j) d -> p b j d", b=B)
        wt = {name: sb("w_" + name, list(ap.shape)) for name, ap in w.items() if name not in ("b2", "wo2", "w_in", "w_a")}
        b2_hi = sb("b2_hi", [P, 1])
        wo2_hi = sb("wo2_hi", [P, D])
        w_gx = sb("w_gx", [P, D])
        w_ga = sb("w_ga", [P, D])
        ident, ones, causal = wt["ident"], wt["ones"], wt["causal"]
        k_row, inv_k, seg = wt["k_row"], wt["inv_k"], wt["seg"]
        one_col = ones[:, 0:1]

        stats = sb("stats", [P, TILES, 6])
        mean = sb("mean", [P, TILES])
        rstd = sb("rstd", [P, TILES])
        var = sb("var", [P, TILES])
        st_a = sb("st_a", [P, TILES])
        st_b = sb("st_b", [P, TILES])
        inv_norm = sb("inv_norm", [P, TILES])
        xn = sb("xn", [P, 2, CT, D])
        xt = sb("xt", [P, 2, CHUNK])
        big_a = sb("big_a", [P, B * T])
        big_b = sb("big_b", [P, B * T])
        big_c = sb("big_c", [P, B * T])
        lg = sb("lg", [P, TILES, E])
        srt = sb("srt", [P, TILES, E])
        e1 = sb("e1", [P, TILES, E])
        e2 = sb("e2", [P, TILES, E])
        e3 = sb("e3", [P, TILES, E])
        e4 = sb("e4", [P, TILES, E])
        gate = sb("gate", [P, TILES, E])
        srt_s = sb("srt_s", [P, 2, CT, E])
        rest_s = sb("rest_s", [P, CT, E])
        gate_s = sb("gate_s", [P, 2, CT, E])
        c1 = sb("c1", [P, 1])
        c1_half = sb("c1_half", [P, 1])
        sp_t = sb("sp_t", [P, 4])
        simn = sb("simn", [P, E])
        sgate = sb("sgate", [P, E])
        sim_t = sb("sim_t", [P, 2, E])
        m8 = sb("m8", [P, 2, CT, 8])
        g1 = sb("g1", [P, CT, E])
        g2 = sb("g2", [P, CT, E])
        g3 = sb("g3", [P, CT, E])
        g4 = sb("g4", [P, CT, E])
        gl = sb("gl", [P, CT, E])
        ge = sb("ge", [P, 2, CT, E])
        gc = sb("gc", [P, 4, CT])
        acc = sb("acc", [P, 2, QKV])
        qkv = sb("qkv", [P, TILES, QKV])
        qk_s = sb("qk_s", [P, 2, CT, 2 * HD])
        q_s = sb("q_s", [HD, 2, P])
        prob = sb("prob", [P, 2, T])
        tx_s, ta_s, y_s, z2_s = (prob[:, m // 2, (m % 2) * 2 * CHUNK:(m % 2 + 1) * 2 * CHUNK].rearrange("p (a n) -> p a n", a=2)
                                 for m in range(4))
        pt_s = sb("pt_s", [P, 2, BANK])
        row_max = sb("row_max", [P, 2, 2])
        row_sum = sb("row_sum", [P, 2, 2])
        att = sb("att", [P, TILES, HD])
        mx_s = sb("mx_s", [P, 2, E, HD])
        h_s = mx_s[:, :, :, :].rearrange("p a e d -> p (a e d)").rearrange("p (j n) -> p j n", j=OC)
        mt_s = sb("mt_s", [P, 2, E * HD])
        at_s = mt_s[0:E, :, 0:CHUNK]
        hq = mt_s[:, :, 0:2 * 3 * D].rearrange("p a (t e) -> p a t e", t=2)
        hp = sb("hp", [P, 3, 2, D])
        hw = sb("hw", [P, 2, 2, 2, HEADS])
        hr = sb("hr", [P, 2, 2, HEADS])
        ot_s = sb("ot_s", [P, 2, 2, D])
        ho = sb("ho", [P, 2, 2, D])

        PS = ctx.enter_context(nc.psum_tensor("PS", [P, 8 * BANK], F32))

        def bank(n, k=1):
            return PS[:, n * BANK:(n + k) * BANK]

        def over_e(a):
            return a.unsqueeze(2).broadcast_to([P, a.shape[1], E])

        x_loaded, w_loaded, bd_clear = sem("x_loaded"), sem("w_loaded"), sem("bd_clear")
        x_done, stored = sem("x_done"), sem("stored")
        n_loads = len(wt) + 2 + 2 * LRU_HEADS

        def carry_wait(engine):
            engine.sem_inc(sem("carried"), 1)

        block = ctx.enter_context(nc.Block())

        @block.sync
        def _(sp):
            sp.dma_start(X[:, :, :], x_in.rearrange("b (j p) d -> p (b j) d", p=P)).then_inc(x_loaded, 16)
            for name in wt:
                sp.dma_start(wt[name][tuple(slice(None) for _ in w[name].shape)], w[name]).then_inc(w_loaded, 16)
            sp.dma_start(b2_hi[HD:P, :], w["b2"]).then_inc(w_loaded, 16)
            sp.dma_start(wo2_hi[HD:P, :], w["wo2"]).then_inc(w_loaded, 16)
            sp.wait_ge(bd_clear, 2)
            bs = D // LRU_HEADS
            for dst, src in ((w_gx, w["w_in"]), (w_ga, w["w_a"])):
                for h in range(LRU_HEADS):
                    sp.dma_start(dst[h * bs:(h + 1) * bs, h * bs:(h + 1) * bs], src[h, :, :]).then_inc(w_loaded, 16)
            sp.wait_ge(x_done, 1)
            sp.dma_start(out.rearrange("b (j p) d -> p (b j) d", p=P), X[:, :, :]).then_inc(stored, 16)
            sp.wait_ge(stored, 16)

        @block.gpsimd
        def _(pool):
            nc.gpsimd.memset(w_gx[:, :], 0.0).then_inc(bd_clear, 1)
            nc.gpsimd.memset(w_ga[:, :], 0.0).then_inc(bd_clear, 1)
            for s in FIRSTS:
                for name in ("xn_ready", "xn_mid"):
                    pool.sem_inc(sem(name, s), HEAD)
            for s in (0,):
                pool.sem_inc(sem("a_ready", s), HEAD)
            for s in (3,):
                for name in ("qk_ready", "q_ready", "mx_ready"):
                    pool.sem_inc(sem(name, s), HEAD)

            def normalise(s):
                C0, N0, G0 = counted(s)
                pool.wait_ge(sem("norm_ready", s), REP[s] + 1)
                with pool.Fori(0, CHUNKS // 2) as i:
                    for par in range(2):
                        c = 2 * i + par
                        tiles = slice(CT * c, CT * c + CT)
                        pool.wait_ge(sem("xt_done", s), free(C0 + c))
                        nc.gpsimd.tensor_tensor(xn[:, par], X[:, bass.ds(CT * c, CT), :],
                                                mean[:, bass.ds(CT * c, CT)].unsqueeze(2).broadcast_to([P, CT, D]),
                                                ALU.subtract).then_inc(sem("xn_mid", s), 1)
                        pool.wait_ge(sem("xn_mid", s), after(C0 + c))
                        nc.gpsimd.tensor_tensor(xn[:, par], xn[:, par],
                                                rstd[:, bass.ds(CT * c, CT)].unsqueeze(2).broadcast_to([P, CT, D]),
                                                ALU.mult).then_inc(sem("xn_ready", s), 1)

            def ffn(s):
                C0, N0, G0 = counted(s)
                normalise(s)
                pool.wait_ge(sem("entmax_done", s), REP[s] + 1)
                with pool.Fori(0, CHUNKS // 2) as i:
                    for par in range(2):
                        c = 2 * i + par
                        pool.wait_ge(sem("at_done", s), free(C0 + c))
                        nc.gpsimd.tensor_copy(gate_s[:, par], gate[:, bass.ds(CT * c, CT), :]).then_inc(sem("a_ready", s), 1)

            def experts(s):
                C0, N0, G0 = counted(s)
                normalise(s)
                pool.wait_ge(sem("qkv_done", s), N0 + TILES)
                with pool.Fori(0, CHUNKS // 2) as i:
                    for par in range(2):
                        c = 2 * i + par
                        pool.wait_ge(sem("qkt_done", s), free(C0 + c))
                        nc.gpsimd.tensor_copy(qk_s[:, par], qkv[:, bass.ds(CT * c, CT), 0:2 * HD]).then_inc(sem("qk_ready", s), 1)
                pool.wait_ge(sem("qt_copied", s), after(C0 + CHUNKS - 1))
                with pool.Fori(0, TILES // 2) as i:
                    for par in range(2):
                        n = 2 * i + par
                        pool.wait_ge(sem("s_done", s), free(N0 + n))
                        nc.gpsimd.tensor_copy(q_s[:, par, :], big_a[0:HD, bass.ds(P * n, P)]).then_inc(sem("q_ready", s), 1)
                pool.wait_ge(sem("att_done", s), after(N0 + TILES - 1))
                with pool.Fori(0, TILES // 2) as i:
                    for par in range(2):
                        n = 2 * i + par
                        pool.wait_ge(sem("mt_done", s), free(N0 + n))
                        nc.gpsimd.tensor_tensor(mx_s[:, par],
                                                gate[:, bass.ds(n, 1), :].rearrange("p o e -> p (o e)").unsqueeze(2).broadcast_to([P, E, HD]),
                                                att[:, bass.ds(n, 1), :].broadcast_to([P, E, HD]),
                                                ALU.mult).then_inc(sem("mx_ready", s), 1)

            def heads(s):
                C0, N0, G0 = counted(s)
                pool.wait_ge(sem("norm_ready", s), REP[s] + 1)
                mean_r = mean[:, :].rearrange("p (b j) -> p b j", b=B)
                rstd_r = rstd[:, :].rearrange("p (b j) -> p b j", b=B)
                with pool.Fori(0, ROW_TILES // 2) as i:
                    for par in range(2):
                        j = 2 * i + par
                        pool.wait_ge(sem("xt_done", s), free(C0 + j))
                        nc.gpsimd.tensor_tensor(xn[:, par, 0:2, :], X_rows[:, :, bass.ds(j, 1), :].rearrange("p b o d -> p b (o d)"),
                                                mean_r[:, :, bass.ds(j, 1)].broadcast_to([P, B, D]),
                                                ALU.subtract).then_inc(sem("xn_mid", s), 1)
                        pool.wait_ge(sem("xn_mid", s), after(C0 + j))
                        nc.gpsimd.tensor_tensor(xn[:, par, 0:2, :], xn[:, par, 0:2, :],
                                                rstd_r[:, :, bass.ds(j, 1)].broadcast_to([P, B, D]),
                                                ALU.mult).then_inc(sem("xn_ready", s), 1)

            for s, stage in enumerate((ffn, normalise, ffn, experts, heads, experts)[:STAGES]):
                stage(s)

        @block.tensor
        def _(pe):
            for s in FIRSTS:
                pe.sem_inc(sem("xt_done", s), HEAD)
            for s in (0,):
                for name in ("lg_done", "u_done", "at_done", "g_done", "z2_done", "out_done"):
                    pe.sem_inc(sem(name, s), HEAD)
            for name in ("gx_done", "ga_done", "yt_done"):
                pe.sem_inc(sem(name, 1), HEAD)
            for s in (3,):
                for name in ("lg_done", "qkt_done", "s_done", "o_done", "mt_done", "out_done"):
                    pe.sem_inc(sem(name, s), HEAD)
            for name in ("hq_done", "ot_done", "out_done"):
                pe.sem_inc(sem(name, 4), HEAD)

            def chunk_loop(pairs, ahead, main):
                ahead(0, 0)
                with pe.Fori(0, pairs - 1) as i:
                    for par in range(2):
                        main(2 * i + par, par, ahead)
                main(2 * pairs - 2, 0, ahead)
                main(2 * pairs - 1, 1, None)

            def transposes(s, source, ready, done, used, dst, rows, count, cols):
                C0 = counted(s)[0]

                def run(c, par):
                    pe.wait_ge(sem(ready, s), after(C0 + c))
                    pe.wait_ge(sem(used, s), free(C0 + c))
                    for t in range(count):
                        last = nc.tensor.transpose(bank(dst + par)[0:cols, t * P:(t + 1) * P], source(par, t), ident[:, :])
                    last.then_inc(sem(done, s), 1)
                return run

            def xn_transposes(s, count=CT):
                return transposes(s, lambda par, t: xn[:, par, t, :], "xn_ready", "xt_done", "xt_copied", 0, P, count, D)

            def ffn(s):
                C0, N0, G0 = counted(s)
                def project(c, par, ahead):
                    if ahead:
                        ahead(c + 1, 1 - par)
                    pe.wait_ge(sem("xt_copied", s), after(C0 + c))
                    pe.wait_ge(sem("lg_copied", s), free(C0 + c))
                    for t in range(CT):
                        last = nc.tensor.matmul(bank(2 + par)[:, t * E:(t + 1) * E], xt[:, par, t * P:(t + 1) * P],
                                                wt["proj"][:, :], start=True, stop=True)
                    last.then_inc(sem("lg_done", s), 1)
                    pe.wait_ge(sem("u_copied", s), free(C0 + c))
                    nc.tensor.matmul(bank(4 + par)[0:R, :], wt["win1"][:, :], xt[:, par, :],
                                     start=True, stop=True).then_inc(sem("u_done", s), 1)

                chunk_loop(CHUNKS // 2, xn_transposes(s), project)

                def rank_gates(c, par, ahead):
                    if ahead:
                        ahead(c + 1, 1 - par)
                    pe.wait_ge(sem("at_copied", s), after(C0 + c))
                    pe.wait_ge(sem("z1_done", s), free(C0 + c))
                    pe.wait_ge(sem("g2_copied", s), free(C0 + c))
                    nc.tensor.matmul(bank(2 + par)[:, :], wt["c12"][:, :], at_s[:, par, :],
                                     start=True, stop=True).then_inc(sem("g_done", s), 1)

                chunk_loop(CHUNKS // 2, transposes(s, lambda par, t: gate_s[:, par, t, :], "a_ready", "at_done", "at_copied", 0, E, CT, E), rank_gates)

                def hidden(c, j):
                    nc.tensor.matmul(bank(j)[:, :], wt["wo1"][:, j * P:(j + 1) * P], big_a[0:R, bass.ds(CHUNK * c, CHUNK)],
                                     start=True, stop=True).then_inc(sem("h_done", s), 1)

                pe.wait_ge(sem("z1_done", s), after(C0 + CHUNKS - 1))
                pe.wait_ge(sem("g2_copied", s), after(C0 + CHUNKS - 1))
                for j in range(OC):
                    hidden(0, j)

                def down(c, par, ahead):
                    pe.wait_ge(sem("z2_ready", s), free(C0 + c))
                    for j in range(OC):
                        pe.wait_ge(sem("gelu_done", s), OC * c + (OC * C0 + j + 1))
                        last = nc.tensor.matmul(bank(4 + par)[R:P, :], wt["win2"][:, j, :], h_s[:, j, :],
                                                start=(j == 0), stop=(j == OC - 1))
                        if j == OC - 1:
                            last.then_inc(sem("z2_done", s), 1)
                        if ahead:
                            hidden(c + 1, j)
                    pe.wait_ge(sem("z2_ready", s), after(C0 + c))
                    pe.wait_ge(sem("x_added", s), free(C0 + c))
                    for t in range(CT):
                        last = nc.tensor.matmul(bank(6 + par)[:, t * D:(t + 1) * D], z2_s[R:P, par, t * P:(t + 1) * P],
                                                wo2_hi[R:P, :], start=True, stop=True)
                    last.then_inc(sem("out_done", s), 1)

                with pe.Fori(0, CHUNKS // 2 - 1) as i:
                    for par in range(2):
                        down(2 * i + par, par, True)
                down(CHUNKS - 2, 0, True)
                down(CHUNKS - 1, 1, False)

            def recurrence(s):
                C0, N0, G0 = counted(s)
                def gates(c, par, ahead):
                    if ahead:
                        ahead(c + 1, 1 - par)
                    pe.wait_ge(sem("xt_copied", s), after(C0 + c))
                    pe.wait_ge(sem("tx_done", s), free(C0 + c))
                    nc.tensor.matmul(bank(2 + par)[:, :], w_gx[:, :], xt[:, par, :], start=True, stop=True).then_inc(sem("gx_done", s), 1)
                    pe.wait_ge(sem("ta_done", s), free(C0 + c))
                    nc.tensor.matmul(bank(4 + par)[:, :], w_ga[:, :], xt[:, par, :], start=True, stop=True).then_inc(sem("ga_done", s), 1)

                chunk_loop(CHUNKS // 2, xn_transposes(s), gates)
                back = transposes(s, lambda par, t: y_s[:, par, t * P:(t + 1) * P], "y_ready", "yt_done", "x_added", 6, P, CT, P)
                with pe.Fori(0, CHUNKS // 2) as i:
                    for par in range(2):
                        back(2 * i + par, par)

            def experts(s):
                C0, N0, G0 = counted(s)
                to_xt = xn_transposes(s)

                def logits(c, par):
                    pe.wait_ge(sem("xt_copied", s), after(C0 + c))
                    pe.wait_ge(sem("lg_copied", s), free(C0 + c))
                    for t in range(CT):
                        last = nc.tensor.matmul(bank(2 + par)[:, t * E:(t + 1) * E], xt[:, par, t * P:(t + 1) * P],
                                                simn[:, :], start=True, stop=True)
                    last.then_inc(sem("lg_done", s), 1)

                def project(c, par, t):
                    for g in range(E // 2):
                        pe.wait_ge(sem("y_used", s), CT * (E // 2) * c + (N0 * (E // 2) + t * (E // 2) + g + 1))
                        nc.tensor.matmul(bank(4 + g % RING)[:, 0:2 * QKV], xt[:, par, t * P:(t + 1) * P],
                                         wt["wqkv"][:, g * 2 * QKV:(g + 1) * 2 * QKV],
                                         start=True, stop=True).then_inc(sem("y_done", s), 1)

                to_xt(0, 0)
                pe.wait_ge(sem("sim_ready"), 1)
                logits(0, 0)

                def main(c, par, ahead):
                    if ahead:
                        to_xt(c + 1, 1 - par)
                    project(c, par, 0)
                    if ahead:
                        logits(c + 1, 1 - par)
                    for t in range(1, CT):
                        project(c, par, t)

                with pe.Fori(0, CHUNKS // 2 - 1) as i:
                    for par in range(2):
                        main(2 * i + par, par, True)
                main(CHUNKS - 2, 0, True)
                main(CHUNKS - 1, 1, False)

                with pe.Fori(0, CHUNKS // 2) as i:
                    for par in range(2):
                        c = 2 * i + par
                        pe.wait_ge(sem("qk_ready", s), after(C0 + c))
                        pe.wait_ge(sem("qt_copied", s), free(C0 + c))
                        pe.wait_ge(sem("kt_copied", s), free(C0 + c))
                        carry_wait(pe)
                        for part in range(2):
                            for t in range(CT):
                                last = nc.tensor.transpose(bank(2 * part + par)[0:HD, t * P:(t + 1) * P],
                                                           qk_s[:, par, t, part * HD:(part + 1) * HD], ident[:, :])
                        last.then_inc(sem("qkt_done", s), 1)

                pe.wait_ge(sem("qt_copied", s), after(C0 + CHUNKS - 1))
                pe.wait_ge(sem("kt_copied", s), after(C0 + CHUNKS - 1))

                def scores(b, i):
                    n = ROW_TILES * b + i
                    pe.wait_ge(sem("q_ready", s), after(N0 + n))
                    pe.wait_ge(sem("exp_done", s), free(N0 + n + 1))
                    carry_wait(pe)
                    for g in range(i // CT + 1):
                        k = min(CT, i + 1 - CT * g)
                        diagonal = g == i // CT
                        last = nc.tensor.matmul(bank(g)[:, 0:k * P], q_s[:, i % 2, :],
                                                big_b[0:HD, bass.ds(T * b + g * CHUNK, k * P)],
                                                start=True, stop=not diagonal)
                        if diagonal:
                            last = nc.tensor.matmul(bank(g)[:, (k - 1) * P:k * P], ident[:, :], causal[:, :],
                                                    start=False, stop=True)
                    last.then_inc(sem("s_done", s), 1)

                groups = [(i, g) for i in range(ROW_TILES) for g in range(i // CT + 1)]

                def turn(b, m):
                    i, g = groups[m]
                    pe.wait_ge(sem("pt_copied", s), free(len(groups) * b + (G0 + m)))
                    for k in range(min(CT, i + 1 - CT * g)):
                        last = nc.tensor.transpose(bank(4 + m % 2)[:, k * P:(k + 1) * P],
                                                   prob[:, i % 2, (CT * g + k) * P:(CT * g + k + 1) * P], ident[:, :])
                    last.then_inc(sem("pt_done", s), 1)

                def mix(b, m):
                    i, g = groups[m]
                    n = ROW_TILES * b + i
                    pe.wait_ge(sem("pt_copied", s), after(len(groups) * b + (G0 + m)))
                    if g == 0:
                        pe.wait_ge(sem("att_done", s), free(N0 + n))
                    for k in range(min(CT, i + 1 - CT * g)):
                        kt = CT * g + k
                        last = nc.tensor.matmul(bank(6 + i % 2)[:, 0:HD], pt_s[:, m % 2, k * P:(k + 1) * P],
                                                qkv[:, bass.ds(ROW_TILES * b + kt, 1), 2 * HD:QKV].rearrange("p o d -> p (o d)"),
                                                start=(kt == 0), stop=(kt == i))
                    if kt == i:
                        last.then_inc(sem("o_done", s), 1)

                with pe.Fori(0, B) as b:
                    scores(b, 0)
                    m = 0
                    for i in range(ROW_TILES):
                        pe.wait_ge(sem("exp_done", s), after(N0 + ROW_TILES * b + i))
                        turn(b, m)
                        if i + 1 < ROW_TILES:
                            scores(b, i + 1)
                        for g in range(i // CT + 1):
                            if g < i // CT:
                                turn(b, m + 1)
                            mix(b, m)
                            m += 1

                pe.wait_ge(sem("att_done", s), after(N0 + TILES - 1))

                def to_mt(n, par):
                    pe.wait_ge(sem("mx_ready", s), after(N0 + n))
                    pe.wait_ge(sem("mt_copied", s), free(N0 + n))
                    for g in range(E * HD // P):
                        last = nc.tensor.transpose(bank(2 * par, 2)[:, g * P:(g + 1) * P],
                                                   mx_s[:, par].rearrange("p e d -> p (e d)")[:, g * P:(g + 1) * P], ident[:, :])
                    last.then_inc(sem("mt_done", s), 1)

                def output(n, par, ahead):
                    if ahead:
                        ahead(n + 1, 1 - par)
                    pe.wait_ge(sem("mt_copied", s), after(N0 + n))
                    pe.wait_ge(sem("x_added", s), free(N0 + n))
                    for g in range(E * HD // P):
                        last = nc.tensor.matmul(bank(4 + par)[:, 0:D], mt_s[:, par, g * P:(g + 1) * P], wt["wo"][:, g, :],
                                                start=(g == 0), stop=(g == E * HD // P - 1))
                    last.then_inc(sem("out_done", s), 1)

                chunk_loop(TILES // 2, to_mt, output)

            def heads(s):
                C0, N0, G0 = counted(s)
                def body(j, par, ahead):
                    if ahead:
                        ahead(j + 1, 1 - par)
                    pe.wait_ge(sem("xt_copied", s), after(C0 + j))
                    pe.wait_ge(sem("hq_copied", s), free(C0 + j + 1))
                    for t in range(2):
                        last = nc.tensor.matmul(bank(2 + t)[:, 0:3 * D], xt[:, par, t * P:(t + 1) * P], wt["w_qkv"][:, :],
                                                start=True, stop=True)
                    last.then_inc(sem("hq_done", s), 1)
                    pe.wait_ge(sem("ho_ready", s), after(C0 + j))
                    pe.wait_ge(sem("ot_copied", s), free(C0 + j))
                    for t in range(2):
                        last = nc.tensor.transpose(bank(4 + par)[:, t * P:(t + 1) * P], ho[:, par, t, :], ident[:, :])
                    last.then_inc(sem("ot_done", s), 1)
                    pe.wait_ge(sem("ot_copied", s), after(C0 + j))
                    pe.wait_ge(sem("x_added", s), free(C0 + j))
                    for t in range(2):
                        last = nc.tensor.matmul(bank(6 + par)[:, t * D:(t + 1) * D], ot_s[:, par, t, :], wt["w_out"][:, :],
                                                start=True, stop=True)
                    last.then_inc(sem("out_done", s), 1)

                chunk_loop(ROW_TILES // 2, xn_transposes(s, 2), body)

            pe.wait_ge(w_loaded, 16 * n_loads)
            pe.wait_ge(sem("sim_sqr"), 1)
            nc.tensor.matmul(bank(7)[:, 0:E], ones[:, :], simn[:, :], start=True, stop=True).then_inc(sem("sim_sq"), 1)
            for s, stage in enumerate((ffn, recurrence, ffn, experts, heads, experts)[:STAGES]):
                stage(s)

        @block.scalar
        def _(act):
            for s in (0,):
                for name in ("xt_copied", "u_copied", "at_copied", "g2_copied"):
                    act.sem_inc(sem(name, s), HEAD)
            for name in ("tx_done", "ta_done", "aa_done", "m_done"):
                act.sem_inc(sem(name, 1), HEAD)
            for s in (3,):
                for name in ("xt_copied", "ge_done", "qt_copied", "exp_done", "pt_copied", "mt_copied"):
                    act.sem_inc(sem(name, s), HEAD)
            for name in ("xt_copied", "hw_done", "ot_copied"):
                act.sem_inc(sem(name, 4), HEAD)
            own = Steps(act, sem("act_steps"))

            def pair_loop(pairs, body):
                with act.Fori(0, pairs) as i:
                    for par in range(2):
                        body(2 * i + par, par)

            def setup():
                act.wait_ge(w_loaded, 16 * n_loads)
                act.wait_ge(sem("sp_abs"), 1)
                own.did(nc.scalar.activation(sp_t[:, 1:2], sp_t[:, 0:1], ACT.Exp, scale=-1.0))
                own.settle()
                nc.scalar.activation(sp_t[:, 2:3], sp_t[:, 1:2], ACT.Ln, bias=one_col, scale=1.0).then_inc(sem("sp_ln"), 1)
                nc.scalar.activation(sim_t[:, 1, :], wt["gates"][:, :], ACT.Tanh, scale=0.5).then_inc(sem("gates_tanh"), 1)
                act.wait_ge(sem("sim_sq"), 1)
                nc.scalar.activation(sim_t[:, 0, :], bank(7)[:, 0:E], ACT.Sqrt).then_inc(sem("sim_norm"), 1)

            def norm(s):
                C0, N0, G0 = counted(s)
                act.wait_ge(sem("var_ready", s), REP[s] + 1)
                if s in (3, 5):
                    own.did(nc.scalar.activation(st_b[:, :], st_b[:, :], ACT.Sqrt))
                nc.scalar.activation(var[:, :], var[:, :], ACT.Sqrt).then_inc(sem("sd_ready", s), 1)

            def copy_xt(s, used, width=CHUNK):
                C0 = counted(s)[0]

                def run(c, par):
                    act.wait_ge(sem("xt_done", s), after(C0 + c))
                    act.wait_ge(sem(used, s), free(C0 + c))
                    nc.scalar.activation(xt[:, par, 0:width], bank(par)[:, 0:width], ACT.Copy).then_inc(sem("xt_copied", s), 1)
                return run

            def ffn(s):
                C0, N0, G0 = counted(s)
                norm(s)
                to_xt = copy_xt(s, "u_done")

                def first(c, par):
                    to_xt(c, par)
                    act.wait_ge(sem("u_done", s), after(C0 + c))
                    nc.scalar.activation(big_a[0:R, bass.ds(CHUNK * c, CHUNK)], bank(4 + par)[0:R, :], ACT.Identity,
                                         bias=wt["b1"][:, :]).then_inc(sem("u_copied", s), 1)

                pair_loop(CHUNKS // 2, first)
                act.wait_ge(sem("lv_ready", s), REP[s] + 1)
                nc.scalar.activation(st_a[:, :], st_a[:, :], ACT.Sqrt).then_inc(sem("ls_ready", s), 1)
                act.wait_ge(sem("delta_ready", s), REP[s] + 1)
                nc.scalar.activation(e4[:, :, :], e4[:, :, :], ACT.Sqrt).then_inc(sem("root_ready", s), 1)

                def second(c, par):
                    act.wait_ge(sem("at_done", s), after(C0 + c))
                    act.wait_ge(sem("g_done", s), free(C0 + c))
                    nc.scalar.activation(at_s[:, par, :], bank(par)[0:E, :], ACT.Copy).then_inc(sem("at_copied", s), 1)
                    act.wait_ge(sem("g_done", s), after(C0 + c))
                    nc.scalar.activation(big_b[R:P, bass.ds(CHUNK * c, CHUNK)], bank(2 + par)[R:P, :], ACT.Copy).then_inc(sem("g2_copied", s), 1)

                pair_loop(CHUNKS // 2, second)
                act.preload_act_table(ACT.Gelu)
                with act.Fori(0, CHUNKS) as c:
                    for j in range(OC):
                        act.wait_ge(sem("h_done", s), OC * c + (OC * C0 + j + 1))
                        nc.scalar.activation(h_s[:, j, :], bank(j)[:, :], ACT.Gelu).then_inc(sem("gelu_done", s), 1)

            def recurrence(s):
                C0, N0, G0 = counted(s)
                norm(s)
                act.preload_act_table(ACT.Exp)

                def gates(c, par):
                    tok = bass.ds(CHUNK * c, CHUNK)
                    act.wait_ge(sem("gx_done", s), after(C0 + c))
                    act.wait_ge(sem("bx_done", s), free(C0 + c))
                    nc.scalar.activation(tx_s[:, par, :], bank(2 + par)[:, :], ACT.Tanh, scale=0.5).then_inc(sem("tx_done", s), 1)
                    act.wait_ge(sem("ga_done", s), after(C0 + c))
                    act.wait_ge(sem("aa_done", s), free(C0 + c))
                    nc.scalar.activation(ta_s[:, par, :], bank(4 + par)[:, :], ACT.Tanh, scale=0.5).then_inc(sem("ta_done", s), 1)
                    act.wait_ge(sem("ta_done", s), after(C0 + c))
                    nc.scalar.activation(big_a[:, tok], ta_s[:, par, :], ACT.Exp, scale=c1_half[:, :], bias=c1_half[:, :])
                    nc.scalar.activation(big_b[:, tok], ta_s[:, par, :], ACT.Exp, scale=c1[:, :], bias=c1[:, :]).then_inc(sem("aa_done", s), 1)

                act.wait_ge(sem("c1_ready"), 1)
                pair_loop(CHUNKS // 2, gates)
                act.preload_act_table(ACT.Sqrt)
                act.wait_ge(sem("aa_done", s), after(C0 + CHUNKS - 1))

                def roots(c, par):
                    tok = bass.ds(CHUNK * c, CHUNK)
                    nc.scalar.activation(big_b[:, tok], big_b[:, tok], ACT.Sqrt, scale=-1.0, bias=one_col).then_inc(sem("m_done", s), 1)

                pair_loop(CHUNKS // 2, roots)

            def experts(s):
                C0, N0, G0 = counted(s)
                norm(s)
                act.preload_act_table(ACT.Exp)

                def expo(c, par):
                    act.wait_ge(sem("gd_ready", s), after(C0 + c))
                    nc.scalar.activation(ge[:, par], ge[:, par], ACT.Exp).then_inc(sem("ge_done", s), 1)

                def copy(c, par):
                    act.wait_ge(sem("xt_done", s), after(C0 + c))
                    act.wait_ge(sem("xt_free", s), free(C0 + c))
                    nc.scalar.activation(xt[:, par, :], bank(par)[:, :], ACT.Copy).then_inc(sem("xt_copied", s), 1)

                def both(c, par):
                    copy(c, par)
                    expo(c, par)

                pair_loop(CHUNKS // 2, both)

                def q_out(c, par):
                    act.wait_ge(sem("qkt_done", s), after(C0 + c))
                    nc.scalar.activation(big_a[0:HD, bass.ds(CHUNK * c, CHUNK)], bank(par)[0:HD, :], ACT.Copy).then_inc(sem("qt_copied", s), 1)

                pair_loop(CHUNKS // 2, q_out)
                groups = [(i, g) for i in range(ROW_TILES) for g in range(i // CT + 1)]

                def expo_row(b, i):
                    n = ROW_TILES * b + i
                    act.wait_ge(sem("max_ready", s), after(N0 + n))
                    act.wait_ge(sem("o_done", s), free(N0 + n))
                    nc.scalar.activation(prob[:, i % 2, 0:(i + 1) * P], PS[:, 0:(i + 1) * P], ACT.Exp, scale=HD ** -0.5,
                                         bias=row_max[:, i % 2, 1:2], accum_out=row_sum[:, i % 2, 0:1]).then_inc(sem("exp_done", s), 1)

                with act.Fori(0, B) as b:
                    expo_row(b, 0)
                    m = 0
                    for i in range(ROW_TILES):
                        for g in range(i // CT + 1):
                            k = min(CT, i + 1 - CT * g)
                            act.wait_ge(sem("pt_done", s), len(groups) * b + (G0 + m + 1))
                            nc.scalar.activation(pt_s[:, m % 2, 0:k * P], bank(4 + m % 2)[:, 0:k * P], ACT.Copy).then_inc(sem("pt_copied", s), 1)
                            m += 1
                        if i + 1 < ROW_TILES:
                            expo_row(b, i + 1)

                def mt_out(n, par):
                    act.wait_ge(sem("mt_done", s), after(N0 + n))
                    act.wait_ge(sem("out_done", s), free(N0 + n))
                    nc.scalar.activation(mt_s[:, par, :], bank(2 * par, 2), ACT.Copy).then_inc(sem("mt_copied", s), 1)

                pair_loop(TILES // 2, mt_out)

            def heads(s):
                C0, N0, G0 = counted(s)
                norm(s)
                act.preload_act_table(ACT.Exp)
                to_xt = copy_xt(s, "hq_done", 2 * P)

                def body(j, par):
                    to_xt(j, par)
                    act.wait_ge(sem("hd_ready", s), after(C0 + j))
                    nc.scalar.activation(hw[:, par], hw[:, par], ACT.Exp).then_inc(sem("hw_done", s), 1)
                    act.wait_ge(sem("ot_done", s), after(C0 + j))
                    act.wait_ge(sem("out_done", s), free(C0 + j))
                    nc.scalar.activation(ot_s[:, par], bank(4 + par)[:, 0:2 * P].rearrange("p (t d) -> p t d", t=2), ACT.Copy).then_inc(sem("ot_copied", s), 1)

                pair_loop(ROW_TILES // 2, body)

            setup()
            for s, stage in enumerate((ffn, recurrence, ffn, experts, heads, experts)[:STAGES]):
                stage(s)

        @block.vector
        def _(dve):
            v = nc.vector
            for s in (0,):
                for name in ("lg_copied", "z1_done", "z2_ready", "x_added"):
                    dve.sem_inc(sem(name, s), HEAD)
            for name in ("xt_copied", "bx_done", "y_ready", "x_added"):
                dve.sem_inc(sem(name, 1), HEAD)
            for s in (3,):
                for name in ("lg_copied", "gd_ready", "kt_copied", "xt_free", "max_ready", "att_done", "x_added"):
                    dve.sem_inc(sem(name, s), HEAD)
                dve.sem_inc(sem("y_used", s), RING)
            for name in ("hq_copied", "hd_ready", "ho_ready", "x_added"):
                dve.sem_inc(sem(name, 4), HEAD)
            own = Steps(dve, sem("dve_steps"))

            def then(instruction):
                own.did(instruction)
                own.settle()

            def pair_loop(pairs, per, body):
                with own.loop(0, pairs, 2 * per) as i:
                    for par in range(2):
                        body(2 * i + par, par)

            def setup():
                dve.wait_ge(w_loaded, 16 * n_loads)
                a = wt["a_param"]
                then(v.tensor_scalar(sp_t[:, 3:4], a[:, :], -1.0, None, ALU.mult))
                v.tensor_tensor(sp_t[:, 0:1], a[:, :], sp_t[:, 3:4], ALU.max).then_inc(sem("sp_abs"), 1)
                dve.wait_ge(sem("sp_ln"), 1)
                then(v.scalar_tensor_tensor(sp_t[:, 3:4], a[:, :], 0.0, sp_t[:, 2:3], ALU.max, ALU.add))
                own.did(v.tensor_scalar(c1_half[:, :], sp_t[:, 3:4], -0.5 * LRU_C, None, ALU.mult))
                v.tensor_scalar(c1[:, :], sp_t[:, 3:4], -LRU_C, None, ALU.mult).then_inc(sem("c1_ready"), 1)
                dve.wait_ge(sem("gates_tanh"), 1)
                own.did(v.tensor_scalar(sgate[:, :], sim_t[:, 1, :], 0.5, 0.5, ALU.mult, ALU.add))
                v.tensor_tensor(simn[:, :], wt["sim"][:, :], wt["sim"][:, :], ALU.mult).then_inc(sem("sim_sqr"), 1)
                dve.wait_ge(sem("sim_norm"), 1)
                then(v.tensor_scalar(sim_t[:, 0, :], sim_t[:, 0, :], 1e-12, None, ALU.max))
                then(v.reciprocal(sim_t[:, 0, :], sim_t[:, 0, :]))
                v.tensor_tensor(simn[:, :], wt["sim"][:, :], sim_t[:, 0, :], ALU.mult).then_inc(sem("sim_ready"), 1)

            def norm(s):
                C0, N0, G0 = counted(s)
                own.settle()
                m_even, m_odd = stats[:, :, 1], stats[:, :, 4]
                own.did(v.tensor_tensor(mean[:, :], m_even, m_odd, ALU.add))
                own.did(v.tensor_tensor(st_a[:, :], m_even, m_odd, ALU.subtract))
                then(v.tensor_tensor(st_b[:, :], stats[:, :, 2], stats[:, :, 5], ALU.add))
                own.did(v.tensor_scalar(mean[:, :], mean[:, :], 0.5, None, ALU.mult))
                then(v.scalar_tensor_tensor(st_a[:, :], st_a[:, :], 0.25, st_a[:, :], ALU.mult, ALU.mult))
                then(v.scalar_tensor_tensor(st_a[:, :], st_b[:, :], 1.0 / D, st_a[:, :], ALU.mult, ALU.add))
                if s in (3, 5):
                    own.did(v.tensor_scalar(st_b[:, :], st_a[:, :], float(D), None, ALU.mult))
                v.tensor_scalar(var[:, :], st_a[:, :], LN_EPS, None, ALU.add).then_inc(sem("var_ready", s), 1)
                dve.wait_ge(sem("sd_ready", s), REP[s] + 1)
                v.reciprocal(rstd[:, :], var[:, :]).then_inc(sem("norm_ready", s), 1)
                if s in (3, 5):
                    dve.wait_ge(sem("norm_ready", s), REP[s] + 1)
                    then(v.tensor_tensor(st_b[:, :], st_b[:, :], rstd[:, :], ALU.mult))
                    then(v.tensor_scalar(st_b[:, :], st_b[:, :], 1e-12, None, ALU.max))
                    then(v.reciprocal(inv_norm[:, :], st_b[:, :]))

            def add_to_x(s, c, par, source, scale, tiles=CT):
                C0 = counted(s)[tiles == 1]
                part = X[:, bass.ds(tiles * c, tiles), :].rearrange("p t d -> p (t d)")
                v.scalar_tensor_tensor(part, source, scale, part, ALU.mult, ALU.add).then_inc(sem("x_added", s), 1)
                dve.wait_ge(sem("x_added", s), after(C0 + c))
                for t in range(tiles):
                    own.did(v.bn_stats(stats[:, bass.ds(tiles * c + t, 1), :].rearrange("p o k -> p (o k)"),
                                       X[:, bass.ds(tiles * c + t, 1), :].rearrange("p o d -> p (o d)")))

            def ffn(s):
                C0, N0, G0 = counted(s)
                norm(s)

                def sort(c, par):
                    some = slice(0, CT * E)
                    dve.wait_ge(sem("lg_done", s), after(C0 + c))
                    own.did(v.tensor_copy(lg[:, bass.ds(CT * c, CT), :], bank(2 + par)[:, some].rearrange("p (t e) -> p t e", t=CT)))
                    for t in range(CT):
                        own.did(v.max(srt_s[:, par, t, 0:8], bank(2 + par)[:, t * E:(t + 1) * E]))
                    own.settle()
                    carry_wait(dve)
                    for t in range(CT):
                        last = v.match_replace(rest_s[:, t, :], srt_s[:, par, t, 0:8], bank(2 + par)[:, t * E:(t + 1) * E], -3e38)
                    last.then_inc(sem("lg_copied", s), 1)
                    dve.wait_ge(sem("lg_copied", s), after(C0 + c))
                    carry_wait(dve)
                    for t in range(CT):
                        own.did(v.max(srt_s[:, par, t, 8:16], rest_s[:, t, :]))
                    own.settle()
                    own.did(v.tensor_copy(srt[:, bass.ds(CT * c, CT), :], srt_s[:, par]))
                    own.settle()

                pair_loop(CHUNKS // 2, 10, sort)

                flat = "p t e -> p (t e)"
                ks = k_row[:, :].unsqueeze(1).broadcast_to([P, TILES, E])
                iks = inv_k[:, :].unsqueeze(1).broadcast_to([P, TILES, E])
                then(v.reduce_sum(mean[:, :], lg[:, :, :], AX.X))
                then(v.tensor_scalar(mean[:, :], mean[:, :], 1.0 / E, None, ALU.mult))
                own.did(v.tensor_tensor(srt[:, :, :], srt[:, :, :], over_e(mean[:, :]), ALU.subtract))
                then(v.tensor_tensor(lg[:, :, :], lg[:, :, :], over_e(mean[:, :]), ALU.subtract))
                then(v.tensor_tensor(e1[:, :, :], lg[:, :, :], lg[:, :, :], ALU.mult))
                then(v.reduce_sum(st_a[:, :], e1[:, :, :], AX.X))
                v.tensor_scalar(st_a[:, :], st_a[:, :], 1.0 / E, LN_EPS, ALU.mult, ALU.add).then_inc(sem("lv_ready", s), 1)
                dve.wait_ge(sem("ls_ready", s), REP[s] + 1)
                then(v.reciprocal(st_a[:, :], st_a[:, :]))
                then(v.tensor_scalar(st_a[:, :], st_a[:, :], 0.5, None, ALU.mult))
                own.did(v.tensor_tensor(srt[:, :, :], srt[:, :, :], over_e(st_a[:, :]), ALU.mult))
                then(v.tensor_tensor(lg[:, :, :], lg[:, :, :], over_e(st_a[:, :]), ALU.mult))
                own.did(v.tensor_copy(st_b[:, :], srt[:, :, 0]))
                own.settle()
                own.did(v.tensor_tensor(lg[:, :, :], lg[:, :, :], over_e(st_b[:, :]), ALU.subtract))
                then(v.tensor_tensor(srt[:, :, :], srt[:, :, :], over_e(st_b[:, :]), ALU.subtract))
                own.did(v.tensor_tensor_scan(e1[:, :, :].rearrange(flat), seg[:, :], srt[:, :, :].rearrange(flat), 0.0, ALU.mult, ALU.add))
                then(v.tensor_tensor(e2[:, :, :], srt[:, :, :], srt[:, :, :], ALU.mult))
                own.did(v.tensor_tensor(e1[:, :, :], e1[:, :, :], iks, ALU.mult))
                then(v.tensor_tensor_scan(e3[:, :, :].rearrange(flat), seg[:, :], e2[:, :, :].rearrange(flat), 0.0, ALU.mult, ALU.add))
                own.did(v.tensor_tensor(e3[:, :, :], e3[:, :, :], iks, ALU.mult))
                then(v.tensor_tensor(e4[:, :, :], e1[:, :, :], e1[:, :, :], ALU.mult))
                then(v.tensor_tensor(e4[:, :, :], e3[:, :, :], e4[:, :, :], ALU.subtract))
                then(v.tensor_tensor(e4[:, :, :], e4[:, :, :], ks, ALU.mult))
                then(v.tensor_scalar(e4[:, :, :], e4[:, :, :], -1.0, 1.0, ALU.mult, ALU.add))
                then(v.tensor_tensor(e4[:, :, :], e4[:, :, :], iks, ALU.mult))
                v.tensor_scalar(e4[:, :, :], e4[:, :, :], 0.0, None, ALU.max).then_inc(sem("delta_ready", s), 1)
                dve.wait_ge(sem("root_ready", s), REP[s] + 1)
                then(v.tensor_tensor(e1[:, :, :], e1[:, :, :], e4[:, :, :], ALU.subtract))
                then(v.tensor_tensor(e2[:, :, :], e1[:, :, :], srt[:, :, :], ALU.is_le))
                then(v.reduce_sum(st_a[:, :], e2[:, :, :], AX.X))
                then(v.tensor_tensor(e2[:, :, :], ks, over_e(st_a[:, :]), ALU.is_equal))
                then(v.tensor_tensor(e2[:, :, :], e2[:, :, :], e1[:, :, :], ALU.mult))
                then(v.reduce_sum(st_b[:, :], e2[:, :, :], AX.X))
                then(v.tensor_tensor(lg[:, :, :], lg[:, :, :], over_e(st_b[:, :]), ALU.subtract))
                then(v.tensor_scalar(lg[:, :, :], lg[:, :, :], 0.0, None, ALU.max))
                v.tensor_tensor(gate[:, :, :], lg[:, :, :], lg[:, :, :], ALU.mult).then_inc(sem("entmax_done", s), 1)

                def first(c, par):
                    dve.wait_ge(sem("g_done", s), after(C0 + c))
                    u = big_a[0:R, bass.ds(CHUNK * c, CHUNK)]
                    v.tensor_tensor(u, bank(2 + par)[0:R, :], u, ALU.mult).then_inc(sem("z1_done", s), 1)

                dve.wait_ge(sem("u_copied", s), after(C0 + CHUNKS - 1))
                pair_loop(CHUNKS // 2, 0, first)
                dve.wait_ge(sem("g2_copied", s), after(C0 + CHUNKS - 1))

                def second(c, par):
                    dve.wait_ge(sem("z2_done", s), after(C0 + c))
                    dve.wait_ge(sem("out_done", s), free(C0 + c))
                    v.scalar_tensor_tensor(z2_s[R:P, par, :], bank(4 + par)[R:P, :], b2_hi[R:P, :],
                                           big_b[R:P, bass.ds(CHUNK * c, CHUNK)], ALU.add, ALU.mult).then_inc(sem("z2_ready", s), 1)
                    dve.wait_ge(sem("out_done", s), after(C0 + c))
                    add_to_x(s, c, par, bank(6 + par), 0.5)

                pair_loop(CHUNKS // 2, CT, second)

            def recurrence(s):
                C0, N0, G0 = counted(s)
                norm(s)

                def gates(c, par):
                    dve.wait_ge(sem("xt_done", s), after(C0 + c))
                    dve.wait_ge(sem("ga_done", s), free(C0 + c))
                    v.tensor_copy(xt[:, par, :], bank(par)).then_inc(sem("xt_copied", s), 1)
                    dve.wait_ge(sem("tx_done", s), after(C0 + c))
                    dve.wait_ge(sem("xt_copied", s), after(C0 + c))
                    v.scalar_tensor_tensor(big_c[:, bass.ds(CHUNK * c, CHUNK)], tx_s[:, par, :], 1.0, xt[:, par, :],
                                           ALU.add, ALU.mult).then_inc(sem("bx_done", s), 1)

                pair_loop(CHUNKS // 2, 0, gates)
                dve.wait_ge(sem("bx_done", s), after(C0 + CHUNKS - 1))
                per_row = T // CHUNK

                with own.loop(0, B, per_row * (1 + CT)) as b:
                    for k in range(per_row):
                        c, par = per_row * b + k, k % 2
                        tok = bass.ds(CHUNK * c, CHUNK)
                        dve.wait_ge(sem("m_done", s), after(C0 + c))
                        then(v.scalar_tensor_tensor(big_c[:, tok], big_c[:, tok], 0.5, big_b[:, tok], ALU.mult, ALU.mult))
                        dve.wait_ge(sem("yt_done", s), free(C0 + c))
                        v.tensor_tensor_scan(y_s[:, par, :], big_a[:, tok], big_c[:, tok],
                                             0.0 if k == 0 else y_s[:, 1 - par, CHUNK - 1:CHUNK],
                                             ALU.mult, ALU.add).then_inc(sem("y_ready", s), 1)
                        dve.wait_ge(sem("y_ready", s), after(C0 + c))
                        dve.wait_ge(sem("yt_done", s), after(C0 + c))
                        add_to_x(s, c, par, bank(6 + par), 1.0)

            def experts(s):
                C0, N0, G0 = counted(s)
                norm(s)
                some = slice(0, CT * E)
                flat = "p t e -> p (t e)"

                def route(c, par):
                    dve.wait_ge(sem("lg_done", s), after(C0 + c))
                    v.tensor_tensor(gl[:, :, :], bank(2 + par)[:, some].rearrange("p (t e) -> p t e", t=CT),
                                    inv_norm[:, bass.ds(CT * c, CT)].unsqueeze(2).broadcast_to([P, CT, E]),
                                    ALU.mult).then_inc(sem("lg_copied", s), 1)
                    dve.wait_ge(sem("lg_copied", s), after(C0 + c))
                    then(v.tensor_tensor(gl[:, :, :], gl[:, :, :], sgate[:, :].unsqueeze(1).broadcast_to([P, CT, E]), ALU.subtract))
                    carry_wait(dve)
                    for t in range(CT):
                        own.did(v.max(m8[:, par, t, :], gl[:, t, :]))
                    own.settle()
                    t1, t2 = m8[:, par, :, 0], m8[:, par, :, 1]
                    own.did(v.tensor_scalar(gc[:, 0, :], t1, 0.0, None, ALU.max))
                    own.did(v.tensor_scalar(g1[:, :, :], gl[:, :, :], 0.0, None, ALU.max))
                    own.did(v.tensor_tensor(gc[:, 1, :], t1, t2, ALU.is_equal))
                    own.did(v.tensor_scalar(gc[:, 2, :], t1, 0.0, None, ALU.is_le))
                    own.settle()
                    v.tensor_tensor(ge[:, par], g1[:, :, :], over_e(gc[:, 0, :]), ALU.subtract).then_inc(sem("gd_ready", s), 1)
                    own.did(v.tensor_scalar(gc[:, 1, :], gc[:, 1, :], 1.0, None, ALU.add))
                    own.did(v.tensor_tensor(g2[:, :, :], gl[:, :, :], over_e(t2), ALU.is_gt))
                    then(v.tensor_tensor(g3[:, :, :], gl[:, :, :], over_e(t2), ALU.is_equal))
                    then(v.tensor_tensor_scan(g4[:, :, :].rearrange(flat), seg[:, some], g3[:, :, :].rearrange(flat), 0.0, ALU.mult, ALU.add))
                    then(v.tensor_tensor(g4[:, :, :], g4[:, :, :], over_e(gc[:, 1, :]), ALU.is_le))
                    then(v.tensor_tensor(g3[:, :, :], g3[:, :, :], g4[:, :, :], ALU.mult))
                    then(v.tensor_tensor(g3[:, :, :], g3[:, :, :], g2[:, :, :], ALU.add))
                    then(v.tensor_tensor(g3[:, :, :], g3[:, :, :], over_e(gc[:, 2, :]), ALU.mult))
                    then(v.scalar_tensor_tensor(g3[:, :, :], gl[:, :, :], 0.0, g3[:, :, :], ALU.is_gt, ALU.add))
                    dve.wait_ge(sem("ge_done", s), after(C0 + c))
                    then(v.tensor_tensor(g3[:, :, :], g3[:, :, :], ge[:, par], ALU.mult))
                    then(v.reduce_sum(gc[:, 3, :], g3[:, :, :], AX.X))
                    then(v.reciprocal(gc[:, 3, :], gc[:, 3, :]))
                    then(v.tensor_tensor(gate_s[:, par], g3[:, :, :], over_e(gc[:, 3, :]), ALU.mult))
                    then(v.tensor_copy(gate[:, bass.ds(CT * c, CT), :], gate_s[:, par]))

                ROUTE = 1 + CT + 4 + 3 + 6 + 5

                def combine(c, par, t):
                    for g in range(E // 2):
                        dve.wait_ge(sem("y_done", s), CT * (E // 2) * c + (N0 * (E // 2) + t * (E // 2) + g + 1))
                        for h in range(2):
                            e = 2 * g + h
                            y = bank(4 + g % RING)[:, h * QKV:(h + 1) * QKV]
                            weight = gate_s[:, par, t, e:e + 1]
                            if g == 0:
                                last = v.tensor_scalar(acc[:, h, :], y, weight, None, ALU.mult)
                            else:
                                last = v.scalar_tensor_tensor(acc[:, h, :], y, weight, acc[:, h, :], ALU.mult, ALU.add)
                            if h == 1:
                                last.then_inc(sem("y_used", s), 1)
                            else:
                                own.did(last)
                        own.settle()
                        dve.wait_ge(sem("y_used", s), CT * (E // 2) * c + (N0 * (E // 2) + t * (E // 2) + g + 1 + RING))
                    v.tensor_tensor(qkv[:, bass.ds(CT * c + t, 1), :].rearrange("p o d -> p (o d)"), acc[:, 0, :], acc[:, 1, :],
                                    ALU.add).then_inc(sem("qkv_done", s), 1)
                    dve.wait_ge(sem("qkv_done", s), CT * c + (N0 + t + 1))

                MIX = E // 2

                def main(c, par, ahead):
                    combine(c, par, 0)
                    if ahead:
                        route(c + 1, 1 - par)
                    for t in range(1, CT):
                        combine(c, par, t)
                    dve.sem_inc(sem("xt_free", s), 1)

                dve.wait_ge(sem("sim_ready"), 1)
                route(0, 0)
                with own.loop(0, CHUNKS // 2 - 1, 2 * (ROUTE + CT * MIX)) as i:
                    for par in range(2):
                        main(2 * i + par, par, True)
                main(CHUNKS - 2, 0, True)
                main(CHUNKS - 1, 1, False)

                def k_out(c, par):
                    dve.wait_ge(sem("qkt_done", s), after(C0 + c))
                    v.tensor_copy(big_b[0:HD, bass.ds(CHUNK * c, CHUNK)], bank(2 + par)[0:HD, :]).then_inc(sem("kt_copied", s), 1)

                pair_loop(CHUNKS // 2, 0, k_out)

                def row_maximum(b, i):
                    n = ROW_TILES * b + i
                    dve.wait_ge(sem("s_done", s), after(N0 + n))
                    then(v.tensor_reduce(row_max[:, i % 2, 0:1], PS[:, 0:(i + 1) * P], AX.X, ALU.max))
                    v.tensor_scalar(row_max[:, i % 2, 1:2], row_max[:, i % 2, 0:1], -(HD ** -0.5), None, ALU.mult).then_inc(sem("max_ready", s), 1)

                with own.loop(0, B, 2 * ROW_TILES) as b:
                    row_maximum(b, 0)
                    for i in range(ROW_TILES):
                        n = ROW_TILES * b + i
                        if i + 1 < ROW_TILES:
                            row_maximum(b, i + 1)
                        dve.wait_ge(sem("exp_done", s), after(N0 + n))
                        then(v.reciprocal(row_sum[:, i % 2, 1:2], row_sum[:, i % 2, 0:1]))
                        dve.wait_ge(sem("o_done", s), after(N0 + n))
                        v.tensor_scalar(att[:, bass.ds(n, 1), :].rearrange("p o d -> p (o d)"), bank(6 + i % 2)[:, 0:HD],
                                        row_sum[:, i % 2, 1:2], None, ALU.mult).then_inc(sem("att_done", s), 1)

                def output(n, par):
                    dve.wait_ge(sem("out_done", s), after(N0 + n))
                    add_to_x(s, n, par, bank(4 + par)[:, 0:D], 0.5, tiles=1)

                pair_loop(TILES // 2, 1, output)

            def heads(s):
                C0, N0, G0 = counted(s)
                norm(s)
                scaling = (D // HEADS) ** -0.5
                hd = D // HEADS

                def by_head(a):
                    return a.rearrange("p (h d) -> p h d", h=HEADS)

                def body(j, par):
                    dve.wait_ge(sem("hq_done", s), after(C0 + j))
                    v.tensor_tensor(hq[:, par], bank(2, 2).rearrange("p (t e) -> p t e", t=2)[:, :, 0:3 * D],
                                    wt["b_qkv"][:, :].unsqueeze(1).broadcast_to([P, 2, 3 * D]), ALU.add).then_inc(sem("hq_copied", s), 1)
                    dve.wait_ge(sem("hq_copied", s), after(C0 + j))
                    q, k, vv = (hq[:, par, :, m * D:(m + 1) * D] for m in range(3))
                    then(v.tensor_tensor(hp[:, 2, 0, :], k[:, 0, :], k[:, 1, :], ALU.subtract))
                    then(v.tensor_tensor(hp[:, 0], q, hp[:, 2, 0, :].unsqueeze(1).broadcast_to([P, 2, D]), ALU.mult))
                    then(v.reduce_sum(hr[:, 0], hp[:, 0].rearrange("p t (h d) -> p t h d", h=HEADS), AX.X))
                    own.did(v.tensor_scalar(hw[:, par, 0], hr[:, 0], scaling, 0.0, ALU.mult, ALU.min))
                    v.tensor_scalar(hw[:, par, 1], hr[:, 0], -scaling, 0.0, ALU.mult, ALU.min).then_inc(sem("hd_ready", s), 1)
                    dve.wait_ge(sem("hw_done", s), after(C0 + j))
                    then(v.tensor_tensor(hr[:, 1], hw[:, par, 0], hw[:, par, 1], ALU.add))
                    then(v.reciprocal(hr[:, 1], hr[:, 1]))
                    for m in range(2):
                        own.did(v.tensor_tensor(hw[:, par, m], hw[:, par, m], hr[:, 1], ALU.mult))
                    own.settle()
                    for m in range(2):
                        for t in range(2):
                            own.did(v.tensor_tensor(by_head(hp[:, m, t, :]), by_head(vv[:, m, :]),
                                                    hw[:, par, m, t, :].unsqueeze(2).broadcast_to([P, HEADS, hd]), ALU.mult))
                    own.settle()
                    dve.wait_ge(sem("ot_done", s), free(C0 + j))
                    v.tensor_tensor(ho[:, par], hp[:, 0], hp[:, 1], ALU.add).then_inc(sem("ho_ready", s), 1)
                    dve.wait_ge(sem("out_done", s), after(C0 + j))
                    part = X_rows[:, :, bass.ds(j, 1), :].rearrange("p b o d -> p b (o d)")
                    then(v.tensor_tensor(part, part, wt["b_out"][:, :].unsqueeze(1).broadcast_to([P, B, D]), ALU.add))
                    v.tensor_tensor(part, bank(6 + par)[:, 0:2 * D].rearrange("p (t d) -> p t d", t=2), part,
                                    ALU.add).then_inc(sem("x_added", s), 1)
                    dve.wait_ge(sem("x_added", s), after(C0 + j))
                    for r in range(B):
                        own.did(v.bn_stats(stats[:, bass.ds(ROW_TILES * r + j, 1), :].rearrange("p o k -> p (o k)"),
                                           X[:, bass.ds(ROW_TILES * r + j, 1), :].rearrange("p o d -> p (o d)")))

                pair_loop(ROW_TILES // 2, 3 + 1 + 4 + 4 + 1 + B, body)

            setup()
            dve.wait_ge(x_loaded, 16)
            with own.loop(0, TILES, 1) as n:
                own.did(v.bn_stats(stats[:, bass.ds(n, 1), :].rearrange("p o k -> p (o k)"),
                                   X[:, bass.ds(n, 1), :].rearrange("p o d -> p (o d)")))
            for s, stage in enumerate((ffn, recurrence, ffn, experts, heads, experts)[:STAGES]):
                stage(s)
            own.settle()
            dve.sem_inc(x_done, 1)


_NAMES = ['L0_attn_x', 'L0_attn_a_param', 'L0_attn_w_in', 'L0_attn_w_a', 'L0_ffn_proj', 'L0_ffn_C1', 'L0_ffn_Win1',
          'L0_ffn_Wout1', 'L0_ffn_C2', 'L0_ffn_Win2', 'L0_ffn_Wout2', 'L1_attn_in_proj_weight', 'L1_attn_in_proj_bias',
          'L1_attn_out_w', 'L1_attn_out_b', 'L1_ffn_sim_matrix', 'L1_ffn_gates', 'L1_ffn_q_proj', 'L1_ffn_k_proj',
          'L1_ffn_v_proj', 'L1_ffn_o_proj']


def laid_out(i):
    k = np.arange(1, E + 1, dtype=np.float32)
    seg = np.ones((TILES, E), np.float32)
    seg[:, 0] = 0.0
    q, kk, v = (i[f"L1_ffn_{n}_proj"] for n in "qkv")
    return {
        "ident": np.eye(P, dtype=np.float32),
        "ones": np.ones((P, P), np.float32),
        "causal": np.triu(np.full((P, P), -1e30, np.float32), 1),
        "k_row": np.broadcast_to(k, (P, E)),
        "inv_k": np.broadcast_to(1 / k, (P, E)),
        "seg": np.broadcast_to(seg.reshape(1, -1), (P, TILES * E)),
        "proj": i["L0_ffn_proj"],
        "c12": np.concatenate([i["L0_ffn_C1"], i["L0_ffn_C2"]], axis=1),
        "win1": i["L0_ffn_Win1"][:D],
        "b1": i["L0_ffn_Win1"][D:].T,
        "wo1": i["L0_ffn_Wout1"].T,
        "win2": i["L0_ffn_Win2"][:O].reshape(OC, P, R).transpose(1, 0, 2),
        "b2": i["L0_ffn_Win2"][O:].T,
        "wo2": i["L0_ffn_Wout2"].T,
        "a_param": i["L0_attn_a_param"].reshape(D, 1),
        "w_in": i["L0_attn_w_in"],
        "w_a": i["L0_attn_w_a"],
        "sim": i["L1_ffn_sim_matrix"],
        "gates": np.broadcast_to(i["L1_ffn_gates"], (P, E)),
        "wqkv": np.concatenate([q, kk, v], axis=2).transpose(1, 0, 2).reshape(D, E * QKV),
        "wo": i["L1_ffn_o_proj"].reshape(E * HD // P, P, D).transpose(1, 0, 2),
        "w_qkv": i["L1_attn_in_proj_weight"].T,
        "b_qkv": np.broadcast_to(i["L1_attn_in_proj_bias"], (P, 3 * D)),
        "w_out": i["L1_attn_out_w"].T,
        "b_out": np.broadcast_to(i["L1_attn_out_b"], (P, D)),
    }


def kernel(**inputs):
    import concourse.bacc as bacc
    from concourse.bass_utils import run_bass_kernel_spmd

    nc = bacc.Bacc("TRN2", target_bir_lowering=False, num_devices=1)
    arrays = {"x_dram": np.ascontiguousarray(inputs["L0_attn_x"])}
    for name, a in laid_out({n: np.asarray(inputs[n]) for n in _NAMES}).items():
        arrays[f"{name}_dram"] = np.ascontiguousarray(a)
    aps = {n: nc.dram_tensor(n, a.shape, F32, kind="ExternalInput").ap() for n, a in arrays.items()}
    out = nc.dram_tensor("out_dram", (B, T, D), F32, kind="ExternalOutput").ap()
    program(nc, aps["x_dram"], out, {n[:-5]: ap for n, ap in aps.items() if n != "x_dram"})
    r = run_bass_kernel_spmd(nc, [arrays], core_ids=[0])
    return r.results[0]["out_dram"]
```

```python
from contextlib import ExitStack, contextmanager

import numpy as np

import concourse.bass as bass
from concourse import mybir

STAGES = 6

B, T, D = 2, 2048, 128
P = 128
TILES = B * T // P
ROW_TILES = T // P
CT = 4
CHUNK = CT * P
CHUNKS = TILES // CT
E, R, O = 16, 64, 512
OC = O // P
BANK = 512
LN_EPS = 1e-5
LRU_C = 8.0
LRU_HEADS = 8
HD = 64
QKV = 3 * HD
ACT_GROUPS = (0, 3, 6)
DVE_GROUPS = tuple(g for g in range(E // 2) if g not in ACT_GROUPS)
ACC = 2 * len(DVE_GROUPS)
PROD = 2 * len(ACT_GROUPS)
YC = CT * E // 2
HEADS = 16
HEAD = 2
RING = 4
UNITS = [(i, k, min(k + 8, i + 1)) for i in range(ROW_TILES) for k in range(0, i + 1, 8)]
PAIRS = ROW_TILES // 2
TURNS = [(a, g) for a in range(PAIRS) for g in range(a + 1)]

KIND = ("ffn", "lru", "ffn", "moe", "mha", "moe")
REP = (0, 0, 1, 0, 0, 1)
FIRSTS = (0, 1, 3, 4)

F32 = mybir.dt.float32
F32R = mybir.dt.float32r
BF16 = mybir.dt.bfloat16
ALU = mybir.AluOpType
ACT = mybir.ActivationFunctionType
AX = mybir.AxisListType


def after(c):
    return c + (1 + HEAD)


def free(c):
    return c + (1 + HEAD - 2)


def counted(s):
    return REP[s] * CHUNKS, REP[s] * TILES


def last_unit(i):
    return max(u for u, unit in enumerate(UNITS) if unit[0] == i)


def schedule():
    order = []
    for a in range(PAIRS + 1):
        mine = [m for m, turn in enumerate(TURNS) if turn[0] == a - 1]
        rest = [("fold", a - 2)] if a >= 2 else []
        rest += [("turn", m) for m in mine[:2]]
        for n, m in enumerate(mine):
            rest += [("turn", t) for t in mine[n + 2:n + 3]] + [("mix", m)]
        half = len(rest) // 2
        for i, part in ((2 * a, rest[:half]), (2 * a + 1, rest[half:])):
            order += [("scores", u) for u, unit in enumerate(UNITS) if unit[0] == i] + part
    return order + [("fold", PAIRS - 1)]


ORDER = schedule()
EXP_DELAY = 2
SLOTS = [event for event in ORDER if event[0] in ("turn", "fold")]
SLOT_BANKS = (4, 5, 7)


def slot_bank(event):
    return SLOT_BANKS[SLOTS.index(event) % len(SLOT_BANKS)]


def slot_before(event):
    n = SLOTS.index(event) - len(SLOT_BANKS)
    return SLOTS[n] if n >= 0 else (None, 0)


def turn_tiles(m):
    return 3 if TURNS[m][0] == TURNS[m][1] else 4


class Steps:

    def __init__(self, engine, semaphore):
        self.engine, self.semaphore, self.base, self.n = engine, semaphore, 0, 0

    def did(self, instruction):
        instruction.then_inc(self.semaphore, 1)
        self.n += 1

    def settle(self):
        self.engine.wait_ge(self.semaphore, self.base + self.n)

    @contextmanager
    def loop(self, start, end, per):
        outer = self.base + self.n
        with self.engine.Fori(start, end) as i:
            self.base, self.n = (i - start) * per + outer, 0
            yield i
            assert self.n == per, f"{self.n} steps in a body of {per}"
        self.base, self.n = outer + (end - start) * per, 0


def program(nc, x_in, out, w):
    ctx = ExitStack()
    with ctx:
        def sb(name, shape, dtype=F32):
            return ctx.enter_context(nc.sbuf_tensor(name, shape, dtype))

        sems = {}

        def sem(name, stage=None):
            name = name if stage is None else f"{KIND[stage]}_{name}"
            if name not in sems:
                sems[name] = ctx.enter_context(nc.semaphore(name))
            return sems[name]

        X = sb("X", [P, TILES, D])
        X_rows = X[:, :, :].rearrange("p (b j) d -> p b j d", b=B)
        early = sb("early", [P, PACKED["early"]])
        late = sb("late", [P, PACKED["late"]])
        wt = {name: {"early": early, "late": late}[pack][lo:hi, at:at + n]
              for name, (pack, lo, hi, at, n) in PLACES.items() if pack != "split"}
        wt["wo"] = wt["wo"].rearrange("p (g d) -> p g d", d=D)
        w_gx = sb("w_gx", [P, D])
        w_ga = sb("w_ga", [P, D])
        ident, ones, causal = wt["ident"], wt["ones"], wt["causal"]
        k_row, inv_k, seg = wt["k_row"], wt["inv_k"], wt["seg"]
        one_col = ones[:, 0:1]
        wqkv_h = sb("wqkv_h", [P, E * QKV], F32R)
        wqkv_l = sb("wqkv_l", [P, E * QKV], F32R)
        wo1_h = sb("wo1_h", [P, O], F32R)
        wo1_l = sb("wo1_l", [P, O], F32R)
        win2_r = sb("win2_r", [P, OC, 2 * R], F32R)
        sim_h = sb("sim_h", [P, E], F32R)
        sim_l = sb("sim_l", [P, E], F32R)
        pick = sb("pick", [2 * 2 * E, E // 2, P], F32R)
        ident_b = sb("ident_b", [P, P], BF16)
        causal_b = sb("causal_b", [P, P], BF16)

        stats = sb("stats", [P, TILES, 6])
        mean = sb("mean", [P, TILES])
        rstd = sb("rstd", [P, TILES])
        var = sb("var", [P, TILES])
        st_a = sb("st_a", [P, TILES])
        st_b = sb("st_b", [P, TILES])
        inv_norm = sb("inv_norm", [P, TILES])
        xn = sb("xn", [P, 2, CT, D])
        gate = sb("gate", [P, TILES, E])
        gate_s = sb("gate_s", [P, 2, CT, E])
        c1 = sb("c1", [P, 1])
        c1_half = sb("c1_half", [P, 1])
        sp_t = sb("sp_t", [P, 4])
        simn = sb("simn", [P, E])
        sgate = sb("sgate", [P, E])
        sim_t = sb("sim_t", [P, 2, E])

        room = ExitStack()

        def room_sb(name, shape, dtype=F32):
            return room.enter_context(nc.sbuf_tensor(name, shape, dtype))

        xt = room_sb("xt", [P, 2, CHUNK])
        big_a = room_sb("big_a", [P, B * T])
        big_b = room_sb("big_b", [P, B * T])
        with ExitStack() as shared:
            big_c = shared.enter_context(nc.sbuf_tensor("big_c", [P, B * T], F32))
        z1_r = room_sb("z1_r", [P, B * T], F32R)
        lg = room_sb("lg", [P, TILES, E])
        srt = room_sb("srt", [P, TILES, E])
        e1 = room_sb("e1", [P, TILES, E])
        e2 = room_sb("e2", [P, TILES, E])
        e3 = room_sb("e3", [P, TILES, E])
        e4 = room_sb("e4", [P, TILES, E])
        srt_s = room_sb("srt_s", [P, 2, CT, E])
        rest_s = room_sb("rest_s", [P, CT, E])
        tx_s = room_sb("tx_s", [P, 2, CHUNK])
        ta_s = room_sb("ta_s", [P, 2, CHUNK])
        y_s = room_sb("y_s", [P, 2, CHUNK])
        z1_s, z2_s = tx_s, y_s
        h_s = room_sb("h_s", [P, OC, CHUNK])
        h_h = room_sb("h_h", [P, OC, CHUNK], F32R)
        h_l = room_sb("h_l", [P, OC, CHUNK], F32R)
        a_s = room_sb("a_s", [P, 2, CT, 4 * E])
        at_r = room_sb("at_r", [4 * E, 2, CHUNK], F32R)
        cc_h = room_sb("cc_h", [4 * E, 4 * R], F32R)
        cc_l = room_sb("cc_l", [4 * E, 4 * R], F32R)
        hq = room_sb("hq", [P, 2, 2, 3 * D])
        hp = room_sb("hp", [P, 3, 2, D])
        hb = room_sb("hb", [P, 3 * D], F32R)
        h_one = room_sb("h_one", [P, P], F32R)
        hw = room_sb("hw", [P, 2, 2, 2, HEADS])
        hr = room_sb("hr", [P, 2, 2, HEADS])
        ot_s = room_sb("ot_s", [P, 2, 2, D])
        ho = room_sb("ho", [P, 2, 2, D])
        room.close()
        m8 = sb("m8", [P, 2, CT, 8])
        g1 = sb("g1", [P, CT, E])
        g2 = sb("g2", [P, CT, E])
        g3 = sb("g3", [P, CT, E])
        g4 = sb("g4", [P, CT, E])
        gl = sb("gl", [P, CT, E])
        ge = sb("ge", [P, 2, CT, E])
        gc = sb("gc", [P, 4, CT])
        xt_h = sb("xt_h", [P, 2, CHUNK], F32R)
        xt_l = sb("xt_l", [P, 2, CHUNK], F32R)
        acc = sb("acc", [P, 2, 2, QKV])
        prod = sb("prod", [P, 2, PROD, QKV])
        qkv = sb("qkv", [P, TILES, QKV])
        q_t = sb("q_t", [P, T], F32R)
        k_h = sb("k_h", [P, T], F32R)
        k_l = sb("k_l", [P, T], F32R)
        v_s = sb("v_s", [P, ROW_TILES, 2 * HD], F32R)
        pt_s = sb("pt_s", [P, 2, BANK], F32R)
        pt = ((xt_h[:, 0], xt_h[:, 1]), (xt_l[:, 0], xt_l[:, 1]), (pt_s[:, 0], pt_s[:, 1]))
        o_s = sb("o_s", [P, 2, 2 * P])
        att_t = sb("att_t", [P, T])
        rw_s = sb("rw_s", [P, 2, CT, 4 * E])
        rw_t = sb("rw_t", [4 * E, 2, CHUNK], F32R)
        row_max = sb("row_max", [P, 4])
        neg_max = sb("neg_max", [P, 4])
        row_sum = sb("row_sum", [P, ROW_TILES, 2])
        inv_sum = sb("inv_sum", [P, ROW_TILES])
        prob = sb("prob", [P, 4, T])
        qk_s = prob[:, 0, :].rearrange("p (a t m w d) -> p a t m w d", a=2, t=CT, m=2, w=2)
        mx_s = prob[:, 1, :].rearrange("p (a n) -> p a n", a=RING)
        prob_flat = prob[:, :, :].rearrange("p a n -> p (a n)")
        wqkv_f = prob_flat[:, 4 * T - E * QKV:]
        split_f = prob_flat[:, 4 * T - E * QKV - PACKED["split"]:4 * T - E * QKV]
        wt |= {name: split_f[lo:hi, at:at + n] for name, (pack, lo, hi, at, n) in PLACES.items() if pack == "split"}
        wt["win2"] = wt["win2"].rearrange("p (j r) -> p j r", j=OC)

        PS = ctx.enter_context(nc.psum_tensor("PS", [P, 8 * BANK], F32))

        def bank(n, k=1):
            return PS[:, n * BANK:(n + k) * BANK]

        def over_e(a):
            return a.unsqueeze(2).broadcast_to([P, a.shape[1], E])

        w_loaded, bd_clear = sem("w_loaded"), sem("bd_clear")
        x_done, stored = sem("x_done"), sem("stored")

        def carry_wait(engine):
            engine.sem_inc(sem("carried"), 1)

        block = ctx.enter_context(nc.Block())

        @block.sync
        def _(sp):
            sp.dma_start(early[:, :], w["early"]).then_inc(w_loaded, 16)
            for r in range(B):
                sp.dma_start(X_rows[:, r], x_in[r].rearrange("(j p) d -> p j d", p=P)).then_inc(sem(f"x_loaded_{r}"), 16)
            sp.dma_start(split_f, w["split"]).then_inc(sem("split_loaded"), 16)
            sp.wait_ge(bd_clear, 2)
            bs = D // LRU_HEADS
            for dst, src in ((w_gx, w["w_in"]), (w_ga, w["w_a"])):
                for h in range(LRU_HEADS):
                    sp.dma_start(dst[h * bs:(h + 1) * bs, h * bs:(h + 1) * bs], src[h, :, :]).then_inc(sem("bd_loaded"), 16)
            sp.dma_start(wqkv_f, w["wqkv"]).then_inc(sem("wqkv_loaded"), 16)
            sp.dma_start(late[:, :], w["late"]).then_inc(sem("late_loaded"), 16)
            sp.wait_ge(x_done, 1)
            sp.dma_start(out.rearrange("b (j p) d -> p (b j) d", p=P), X[:, :, :]).then_inc(stored, 16)
            sp.wait_ge(stored, 16)

        @block.gpsimd
        def _(pool):
            nc.gpsimd.memset(w_gx[:, :], 0.0).then_inc(bd_clear, 1)
            nc.gpsimd.memset(w_ga[:, :], 0.0).then_inc(bd_clear, 1)
            for s in FIRSTS:
                for name in ("xn_ready", "xn_mid"):
                    pool.sem_inc(sem(name, s), HEAD)
            for name in ("x_biased", "hv_done"):
                pool.sem_inc(sem(name, 4), HEAD)
            for s in (0,):
                pool.sem_inc(sem("a_ready", s), HEAD)
            for s in (3,):
                for name in ("qkv_done", "rw_ready"):
                    pool.sem_inc(sem(name, s), HEAD)

            def normalised(s, c, par):
                C0 = counted(s)[0]
                pool.wait_ge(sem("xt_done", s), free(C0 + c))
                nc.gpsimd.tensor_tensor(xn[:, par], X[:, bass.ds(CT * c, CT), :],
                                        mean[:, bass.ds(CT * c, CT)].unsqueeze(2).broadcast_to([P, CT, D]),
                                        ALU.subtract).then_inc(sem("xn_mid", s), 1)
                pool.wait_ge(sem("xn_mid", s), after(C0 + c))
                nc.gpsimd.tensor_tensor(xn[:, par], xn[:, par],
                                        rstd[:, bass.ds(CT * c, CT)].unsqueeze(2).broadcast_to([P, CT, D]),
                                        ALU.mult).then_inc(sem("xn_ready", s), 1)

            def normalise(s):
                pool.wait_ge(sem("norm_ready", s), REP[s] + 1)
                with pool.Fori(0, CHUNKS // 2) as i:
                    for par in range(2):
                        normalised(s, 2 * i + par, par)

            def ffn(s):
                C0, N0 = counted(s)
                normalise(s)
                own.did(nc.gpsimd.memset(a_s[:, :, :, :], 0.0))
                if s == 0:
                    pool.wait_ge(sem("wqkv_loaded"), 16)
                    own.did(nc.gpsimd.tensor_copy(wqkv_h[:, :], wqkv_f))
                    own.settle()
                    nc.gpsimd.tensor_tensor(wqkv_l[:, :], wqkv_f, wqkv_h[:, :].bitcast(F32), ALU.subtract).then_inc(sem("wqkv_split"), 1)
                own.settle()
                pool.wait_ge(sem("entmax_done", s), REP[s] + 1)
                with pool.Fori(0, CHUNKS // 2) as i:
                    for par in range(2):
                        c = 2 * i + par
                        pool.wait_ge(sem("at_done", s), free(C0 + c))
                        for at in (0, 2 * E):
                            last = nc.gpsimd.tensor_copy(a_s[:, par, :, at:at + E], gate[:, bass.ds(CT * c, CT), :])
                        last.then_inc(sem("a_ready", s), 1)
                with pool.Fori(0, CHUNKS) as c:
                    for j in range(OC - 1):
                        pool.wait_ge(sem("h_hi", s), OC * c + (OC * C0 + j + 1))
                        nc.gpsimd.tensor_tensor(h_l[:, j, :], h_s[:, j, :], h_h[:, j, :].bitcast(F32), ALU.subtract).then_inc(sem("h_lo", s), 1)

            def experts(s):
                C0, N0 = counted(s)
                pool.wait_ge(sem("norm_ready", s), REP[s] + 1)
                for par in range(2):
                    normalised(s, par, par)
                own.did(nc.gpsimd.memset(rw_s[:, :, :, :], 0.0))
                own.did(nc.gpsimd.memset(row_sum[:, :, :], 0.0))
                own.settle()

                def gather(c, par, t):
                    n, q = CT * c + t, t % 2
                    pool.wait_ge(sem("prod_done", s), PROD * CT * c + (PROD * (N0 + t) + 2 * PROD))
                    own.did(nc.gpsimd.tensor_tensor(prod[:, q, 2:4, :], prod[:, q, 2:4, :], prod[:, q, 4:6, :], ALU.add))
                    own.settle()
                    pool.wait_ge(sem("acc_done", s), ACC * CT * c + (ACC * (N0 + t) + 2 * ACC))
                    own.did(nc.gpsimd.tensor_tensor(prod[:, q, 2:4, :], prod[:, q, 2:4, :], acc[:, q, :, :], ALU.add))
                    own.settle()
                    nc.gpsimd.tensor_tensor(qkv[:, bass.ds(n, 1), :].rearrange("p o d -> p (o d)"), prod[:, q, 2, :], prod[:, q, 3, :],
                                            ALU.add).then_inc(sem("qkv_done", s), 1)

                def chunk(c, par, ahead):
                    for t in range(CT):
                        gather(c, par, t)
                        if ahead and t == 1:
                            normalised(s, c + 2, par)

                with own.loop(0, CHUNKS // 2 - 1, 4 * CT) as i:
                    for par in range(2):
                        chunk(2 * i + par, par, True)
                for par in range(2):
                    chunk(CHUNKS - 2 + par, par, False)
                per_row = T // CHUNK
                with pool.Fori(0, B) as b:
                    pool.wait_ge(sem("rw_scaled", s), REP[s] * B + b + 1)
                    for k in range(per_row):
                        c, par = per_row * b + k, k % 2
                        pool.wait_ge(sem("rwt_done", s), free(C0 + c))
                        for at in (0, 2 * E):
                            last = nc.gpsimd.tensor_copy(rw_s[:, par, :, at:at + E], gate[:, bass.ds(CT * c, CT), :])
                        last.then_inc(sem("rw_ready", s), 1)

            def heads(s):
                C0, N0 = counted(s)
                pool.wait_ge(sem("late_loaded"), 16)
                pool.wait_ge(sem("norm_ready", s), REP[s] + 1)
                mean_r = mean[:, :].rearrange("p (b j) -> p b j", b=B)
                rstd_r = rstd[:, :].rearrange("p (b j) -> p b j", b=B)

                def normalised_pair(j, par):
                    pool.wait_ge(sem("xt_done", s), free(C0 + j))
                    part = X_rows[:, :, bass.ds(j, 1), :].rearrange("p b o d -> p b (o d)")
                    nc.gpsimd.tensor_tensor(xn[:, par, 0:2, :], part, mean_r[:, :, bass.ds(j, 1)].broadcast_to([P, B, D]),
                                            ALU.subtract).then_inc(sem("xn_mid", s), 1)
                    pool.wait_ge(sem("xn_mid", s), after(C0 + j))
                    nc.gpsimd.tensor_tensor(xn[:, par, 0:2, :], xn[:, par, 0:2, :], rstd_r[:, :, bass.ds(j, 1)].broadcast_to([P, B, D]),
                                            ALU.mult).then_inc(sem("xn_ready", s), 1)
                    nc.gpsimd.tensor_tensor(part, part, wt["b_out"][:, :].unsqueeze(1).broadcast_to([P, B, D]),
                                            ALU.add).then_inc(sem("x_biased", s), 1)

                def second_value(j, par):
                    pool.wait_ge(sem("hv_ready", s), after(C0 + j))
                    value = hq[:, par, 1, 2 * D:3 * D].rearrange("p (h d) -> p h d", h=HEADS).unsqueeze(1)
                    nc.gpsimd.tensor_tensor(hp[:, 1].rearrange("p t (h d) -> p t h d", h=HEADS),
                                            value.broadcast_to([P, 2, HEADS, D // HEADS]),
                                            hw[:, par, 1].unsqueeze(3).broadcast_to([P, 2, HEADS, D // HEADS]),
                                            ALU.mult).then_inc(sem("hv_done", s), 1)

                for j in range(3):
                    normalised_pair(j, j % 2)
                normalised_pair(3, 1)
                second_value(0, 0)
                with pool.Fori(0, ROW_TILES // 2 - 2) as i:
                    for n in (1, 2):
                        normalised_pair(2 * i + (n + 3), 1 - n % 2)
                        second_value(2 * i + n, n % 2)
                for j in range(ROW_TILES - 3, ROW_TILES):
                    second_value(j, j % 2)

            own = Steps(pool, sem("pool_steps"))
            for s, stage in enumerate((ffn, normalise, ffn, experts, heads, experts)[:STAGES]):
                stage(s)

        @block.tensor
        def _(pe):
            for s in FIRSTS:
                pe.sem_inc(sem("xt_done", s), HEAD)
            for s in (0,):
                for name in ("lg_done", "u_done", "at_done", "g_done", "z2_done", "out_done"):
                    pe.sem_inc(sem(name, s), HEAD)
            for name in ("gx_done", "ga_done", "yt_done"):
                pe.sem_inc(sem(name, 1), HEAD)
            for s in (3,):
                for name in ("lg_done", "qkt_done", "s_done", "pt_done", "ot_done", "at_done", "rwt_done"):
                    pe.sem_inc(sem(name, s), HEAD)
                pe.sem_inc(sem("y_done", s), 2 * YC)
                pe.sem_inc(sem("bc_done", s), E // 2)
                pe.sem_inc(sem("og_done", s), E // 2)
            for name in ("hq_done", "ot_done", "out_done"):
                pe.sem_inc(sem(name, 4), HEAD)

            def chunk_loop(pairs, ahead, main):
                ahead(0, 0)
                with pe.Fori(0, pairs - 1) as i:
                    for par in range(2):
                        main(2 * i + par, par, ahead)
                main(2 * pairs - 2, 0, ahead)
                main(2 * pairs - 1, 1, None)

            def transposes(s, source, ready, done, used, dst, rows, count, cols):
                C0 = counted(s)[0]

                def run(c, par):
                    pe.wait_ge(sem(ready, s), after(C0 + c))
                    pe.wait_ge(sem(used, s), free(C0 + c))
                    for t in range(count):
                        last = nc.tensor.transpose(bank(dst + par)[0:cols, t * P:(t + 1) * P], source(par, t), ident[:, :])
                    last.then_inc(sem(done, s), 1)
                return run

            def xn_transposes(s, count=CT):
                return transposes(s, lambda par, t: xn[:, par, t, :], "xn_ready", "xt_done", "xt_copied", 0, P, count, D)

            def ffn(s):
                C0, N0 = counted(s)
                def project(c, par, ahead):
                    if ahead:
                        ahead(c + 1, 1 - par)
                    pe.wait_ge(sem("xt_copied", s), after(C0 + c))
                    pe.wait_ge(sem("lg_copied", s), free(C0 + c))
                    for t in range(CT):
                        last = nc.tensor.matmul(bank(2 + par)[:, t * E:(t + 1) * E], xt[:, par, t * P:(t + 1) * P],
                                                wt["proj"][:, :], start=True, stop=True)
                    last.then_inc(sem("lg_done", s), 1)
                    pe.wait_ge(sem("u_copied", s), free(C0 + c))
                    nc.tensor.matmul(bank(4 + par)[:, :], wt["win1"][:, :], xt[:, par, :],
                                     start=True, stop=True).then_inc(sem("u_done", s), 1)

                chunk_loop(CHUNKS // 2, xn_transposes(s), project)

                def turn_weights(c, par):
                    pe.wait_ge(sem("a_ready", s), after(C0 + c))
                    pe.wait_ge(sem("at_lo", s), free(C0 + c))
                    carry_wait(pe)
                    for t in range(CT):
                        last = nc.tensor.transpose(bank(par)[0:4 * E, t * P:(t + 1) * P], a_s[:, par, t, :], ident[:, :])
                    last.then_inc(sem("at_done", s), 1)

                def rank_gates(c, par, ahead):
                    if ahead:
                        ahead(c + 1, 1 - par)
                    pe.wait_ge(sem("at_lo", s), after(C0 + c))
                    pe.wait_ge(sem("z1_done", s), free(C0 + c))
                    pe.wait_ge(sem("g2_copied", s), free(C0 + c))
                    for layer in (1, 0):
                        for m, part in enumerate((cc_h, cc_l)):
                            last = nc.tensor.matmul(bank(2 + 2 * layer + par)[:, :], part[:, 2 * R * layer:2 * R * (layer + 1)], at_r[:, par, :],
                                                    start=(m == 0), stop=(m == 1))
                    last.then_inc(sem("g_done", s), 1)

                pe.wait_ge(sem("u_copied", s), after(C0 + CHUNKS - 1))

                pe.wait_ge(sem("cc_ready", s), REP[s] + 1)
                chunk_loop(CHUNKS // 2, turn_weights, rank_gates)

                def hidden(c, j):
                    for m, part in enumerate((wo1_h, wo1_l)):
                        last = nc.tensor.matmul(bank(j)[:, :], part[:, j * P:(j + 1) * P], z1_r[:, bass.ds(CHUNK * c, CHUNK)],
                                                start=(m == 0), stop=(m == 1))
                    last.then_inc(sem("h_done", s), 1)

                pe.wait_ge(sem("z1_done", s), after(C0 + CHUNKS - 1))
                pe.wait_ge(sem("g2_copied", s), after(C0 + CHUNKS - 1))
                for j in range(OC):
                    hidden(0, j)

                def output(c, par):
                    pe.wait_ge(sem("z2_ready", s), after(C0 + c))
                    pe.wait_ge(sem("x_added", s), free(C0 + c))
                    for t in range(CT):
                        last = nc.tensor.matmul(bank(6 + par)[:, t * D:(t + 1) * D], z2_s[:, par, t * P:(t + 1) * P],
                                                wt["wo2"][:, :], start=True, stop=True)
                    last.then_inc(sem("out_done", s), 1)

                def down(c, par, ahead, behind):
                    pe.wait_ge(sem("z2_ready", s), free(C0 + c))
                    for j in range(OC):
                        if j < OC - 1:
                            pe.wait_ge(sem("h_lo", s), (OC - 1) * c + ((OC - 1) * C0 + j + 1))
                        else:
                            pe.wait_ge(sem("h_lo_last", s), C0 + c + 1)
                        for m, part in enumerate((h_h, h_l)):
                            last = nc.tensor.matmul(bank(4 + par)[:, :], win2_r[:, j, :], part[:, j, :],
                                                    start=(j == 0 and m == 0), stop=(j == OC - 1 and m == 1))
                        if j == OC - 1:
                            last.then_inc(sem("z2_done", s), 1)
                        if ahead:
                            hidden(c + 1, j)
                        if behind and j == 1:
                            output(c - 1, 1 - par)

                down(0, 0, True, False)
                with pe.Fori(0, CHUNKS // 2 - 1) as i:
                    for n in (1, 2):
                        down(2 * i + n, n % 2, True, True)
                down(CHUNKS - 1, 1, False, True)
                output(CHUNKS - 1, 1)

            def recurrence(s):
                C0, N0 = counted(s)
                pe.wait_ge(sem("bd_loaded"), 16 * 2 * LRU_HEADS)

                def gates(c, par, ahead):
                    if ahead:
                        ahead(c + 1, 1 - par)
                    pe.wait_ge(sem("xt_copied", s), after(C0 + c))
                    pe.wait_ge(sem("tx_done", s), free(C0 + c))
                    nc.tensor.matmul(bank(2 + par)[:, :], w_gx[:, :], xt[:, par, :], start=True, stop=True).then_inc(sem("gx_done", s), 1)
                    pe.wait_ge(sem("ta_done", s), free(C0 + c))
                    nc.tensor.matmul(bank(4 + par)[:, :], w_ga[:, :], xt[:, par, :], start=True, stop=True).then_inc(sem("ga_done", s), 1)

                chunk_loop(CHUNKS // 2, xn_transposes(s), gates)
                back = transposes(s, lambda par, t: y_s[:, par, t * P:(t + 1) * P], "y_ready", "yt_done", "x_added", 6, P, CT, P)
                with pe.Fori(0, CHUNKS // 2) as i:
                    for par in range(2):
                        back(2 * i + par, par)

            def experts(s):
                C0, N0 = counted(s)
                to_xt = transposes(s, lambda par, t: xn[:, par, t, :], "xn_ready", "xt_done", "xt_lo", 0, P, CT, D)

                def logits(c, par):
                    pe.wait_ge(sem("xt_lo", s), after(C0 + c))
                    pe.wait_ge(sem("lg_copied", s), free(C0 + c))
                    for t in range(CT):
                        tok = slice(t * P, (t + 1) * P)
                        for m, (x_part, w_part) in enumerate(((xt_h, sim_h), (xt_h, sim_l), (xt_l, sim_h))):
                            last = nc.tensor.matmul(bank(2 + par)[:, t * E:(t + 1) * E], x_part[:, par, tok], w_part[:, :],
                                                    start=(m == 0), stop=(m == 2))
                    last.then_inc(sem("lg_done", s), 1)

                def bank_left(c, t, g):
                    other = g - RING if g >= RING else g + RING
                    mine, name, per = (ACT_GROUPS, "prod_done", PROD) if other in ACT_GROUPS else (DVE_GROUPS, "acc_done", ACC)
                    this_tile = per if g >= RING else 0
                    pe.wait_ge(sem(name, s), per * CT * c + (per * (N0 + t) + this_tile + 2 * (mine.index(other) + 1)))

                def project(c, par, t):
                    tok = slice(t * P, (t + 1) * P)
                    for g in range(E // 2):
                        bank_left(c, t, g)
                        cols = slice(g * 2 * QKV, (g + 1) * 2 * QKV)
                        for m, (x_part, w_part) in enumerate(((xt_h, wqkv_h), (xt_h, wqkv_l), (xt_l, wqkv_h))):
                            last = nc.tensor.matmul(bank(4 + g % RING)[:, 0:2 * QKV], x_part[:, par, tok], w_part[:, cols],
                                                    start=(m == 0), stop=(m == 2))
                        last.then_inc(sem("y_done", s), 1)

                to_xt(0, 0)
                pe.wait_ge(sem("sim_ready"), 1)
                logits(0, 0)
                pe.wait_ge(sem("wqkv_split"), 1)

                def main(c, par, ahead):
                    if ahead:
                        to_xt(c + 1, 1 - par)
                    project(c, par, 0)
                    if ahead:
                        logits(c + 1, 1 - par)
                    project(c, par, 1)
                    project(c, par, 2)
                    project(c, par, 3)

                with pe.Fori(0, CHUNKS // 2 - 1) as i:
                    for par in range(2):
                        main(2 * i + par, par, True)
                main(CHUNKS - 2, 0, True)
                main(CHUNKS - 1, 1, False)

                per_row = T // CHUNK
                with pe.Fori(0, B) as b:
                    U0, M0, A0 = (REP[s] * B + b) * len(UNITS), (REP[s] * B + b) * len(TURNS), (REP[s] * B + b) * PAIRS

                    for k in range(per_row):
                        c, par = per_row * b + k, k % 2
                        pe.wait_ge(sem("qk_ready", s), after(C0 + c))
                        pe.wait_ge(sem("qt_lo", s), free(C0 + c))
                        pe.wait_ge(sem("kt_lo", s), free(C0 + c))
                        for part in range(2):
                            for t in range(CT):
                                last = nc.tensor.transpose(bank(2 * part + par)[:, t * P:(t + 1) * P],
                                                           qk_s[:, par, t, part].rearrange("p a d -> p (a d)"), ident[:, :])
                        last.then_inc(sem("qkt_done", s), 1)
                    pe.wait_ge(sem("qt_lo", s), after(C0 + per_row * b + per_row - 1))
                    pe.wait_ge(sem("kt_lo", s), after(C0 + per_row * b + per_row - 1))
                    pe.wait_ge(sem("v_lo", s), REP[s] * B + b + 1)

                    def scores(u):
                        i, k0, k1 = UNITS[u]
                        pe.wait_ge(sem("exp_done", s), free(U0 + u))
                        for k in range(k0, k1, CT):
                            n = min(CT, k1 - k)
                            dst = bank(2 * (u % 2) + (k - k0) // CT)
                            diagonal = k + n == i + 1
                            for m, k_part in enumerate((k_h, k_l)):
                                last = nc.tensor.matmul(dst[:, 0:n * P], q_t[:, i * P:(i + 1) * P], k_part[:, k * P:(k + n) * P],
                                                        start=(m == 0), stop=(m == 1 and not diagonal))
                            if diagonal:
                                last = nc.tensor.matmul(dst[:, (n - 1) * P:n * P], ident_b[:, :], causal_b[:, :], start=False, stop=True)
                        last.then_inc(sem("s_done", s), 1)

                    def slot_left(event):
                        kind, n = slot_before(event)
                        if kind == "turn":
                            pe.wait_ge(sem("pt_lo", s), after(M0 + n))
                        if kind == "fold":
                            pe.wait_ge(sem("at_copied", s), after(A0 + n))

                    def turn(m):
                        a, g = TURNS[m]
                        if g == 0:
                            pe.wait_ge(sem("exp_done", s), after(U0 + last_unit(2 * a + 1)))
                        slot_left(("turn", m))
                        at = 0
                        for k in (2 * g, 2 * g + 1):
                            for i in (2 * a, 2 * a + 1):
                                if k <= i:
                                    last = nc.tensor.transpose(bank(slot_bank(("turn", m)))[:, at:at + P], prob[:, i % 4, k * P:(k + 1) * P], ident[:, :])
                                    at += P
                        last.then_inc(sem("pt_done", s), 1)

                    def mix(m):
                        a, g = TURNS[m]
                        pe.wait_ge(sem("pt_lo", s), after(M0 + m))
                        if g == 0:
                            pe.wait_ge(sem("ot_copied", s), free(A0 + a + 1))
                        at = 0
                        for k in (2 * g, 2 * g + 1):
                            n = 2 * P if k <= 2 * a else P
                            for m2, part in enumerate(pt[m % 3]):
                                last = nc.tensor.matmul(bank(6)[:, 2 * P - n:2 * P], v_s[:, k, :], part[:, at:at + n],
                                                        start=(k == 0 and m2 == 0), stop=(k == 2 * a + 1 and m2 == 1))
                            at += n
                        if g == a:
                            last.then_inc(sem("ot_done", s), 1)

                    def fold(a):
                        pe.wait_ge(sem("ot_copied", s), after(A0 + a))
                        slot_left(("fold", a))
                        nc.tensor.matmul(bank(slot_bank(("fold", a)))[:, 0:2 * P], wt["fold"], o_s[:, a % 2, :],
                                         start=True, stop=True).then_inc(sem("at_done", s), 1)

                    for kind, n in ORDER:
                        {"scores": scores, "turn": turn, "mix": mix, "fold": fold}[kind](n)

                    pe.wait_ge(sem("at_copied", s), after(A0 + PAIRS - 1))

                    def weights(k):
                        c, par = per_row * b + k, k % 2
                        pe.wait_ge(sem("rw_ready", s), after(C0 + c))
                        pe.wait_ge(sem("rwt_lo", s), free(C0 + c))
                        carry_wait(pe)
                        for t in range(CT):
                            last = nc.tensor.transpose(bank(par)[0:4 * E, t * P:(t + 1) * P], rw_s[:, par, t, :], ident[:, :])
                        last.then_inc(sem("rwt_done", s), 1)

                    def spread(k, g):
                        n = (E // 2) * (C0 + per_row * b)
                        if g == 0:
                            pe.wait_ge(sem("rwt_lo", s), after(C0 + per_row * b + k))
                        pe.wait_ge(sem("mx_done", s), n + ((E // 2) * (k + 1) + g + 1 - RING))
                        nc.tensor.matmul(bank(2 + g % RING)[:, :], pick[:, g, :], rw_t[:, k % 2, :], start=True, stop=True)\
                            .then_inc(sem("bc_done", s), 1)

                    weights(0)
                    for k in range(per_row):
                        c, par = per_row * b + k, k % 2
                        n = (E // 2) * (C0 + per_row * b)
                        pe.wait_ge(sem("x_added", s), free(C0 + c))
                        if k == 0:
                            spread(k, 0)
                            spread(k, 1)
                        for g in range(E // 2):
                            if g < E // 2 - 2:
                                spread(k, g + 2)
                            elif k + 1 < per_row:
                                spread(k + 1, g + 2 - E // 2)
                            if g == 1 and k + 1 < per_row:
                                weights(k + 1)
                            pe.wait_ge(sem("mx_done", s), n + ((E // 2) * (k + 1) + g + 1))
                            for t in range(CT):
                                last = nc.tensor.matmul(bank(6 + par)[:, t * D:(t + 1) * D], mx_s[:, g % RING, t * P:(t + 1) * P],
                                                        wt["wo"][:, g, :], start=(g == 0 and t == 0), stop=(g == E // 2 - 1 and t == CT - 1),
                                                        skip_group_check=True)
                            last.then_inc(sem("og_done", s), 1)

            def heads(s):
                C0, N0 = counted(s)
                def to_xt(j, par):
                    pe.wait_ge(sem("xn_ready", s), after(C0 + j))
                    pe.wait_ge(sem("xt_copied", s), free(C0 + j + 1))
                    for t in range(2):
                        last = nc.tensor.transpose(bank(0)[:, t * P:(t + 1) * P], xn[:, par, t, :], ident[:, :])
                    last.then_inc(sem("xt_done", s), 1)

                def project(j, par):
                    pe.wait_ge(sem("xt_copied", s), after(C0 + j))
                    pe.wait_ge(sem("hq_copied", s), free(C0 + j))
                    for t in range(2):
                        nc.tensor.matmul(bank(2 + 2 * par + t)[:, 0:3 * D], xt[:, par, t * P:(t + 1) * P], wt["w_qkv"][:, :],
                                         start=True, stop=False)
                        last = nc.tensor.matmul(bank(2 + 2 * par + t)[:, 0:3 * D], h_one[:, :], hb[:, :], start=False, stop=True)
                    last.then_inc(sem("hq_done", s), 1)

                def attended(j, par):
                    pe.wait_ge(sem("ho_ready", s), after(C0 + j))
                    pe.wait_ge(sem("ot_copied", s), free(C0 + j + 1))
                    for t in range(2):
                        last = nc.tensor.transpose(bank(1)[:, t * P:(t + 1) * P], ho[:, par, t, :], ident[:, :])
                    last.then_inc(sem("ot_done", s), 1)

                def output(j, par):
                    pe.wait_ge(sem("ot_copied", s), after(C0 + j))
                    pe.wait_ge(sem("x_added", s), free(C0 + j))
                    for t in range(2):
                        last = nc.tensor.matmul(bank(6 + par)[:, t * D:(t + 1) * D], ot_s[:, par, t, :], wt["w_out"][:, :],
                                                start=True, stop=True)
                    last.then_inc(sem("out_done", s), 1)

                to_xt(0, 0)
                to_xt(1, 1)
                pe.wait_ge(sem("hb_ready"), 1)
                project(0, 0)
                to_xt(2, 0)
                project(1, 1)
                to_xt(3, 1)
                project(2, 0)
                attended(0, 0)
                with pe.Fori(0, ROW_TILES // 2 - 2) as i:
                    for n in (1, 2):
                        j = 2 * i + n
                        to_xt(j + 3, 1 - n % 2)
                        project(j + 2, n % 2)
                        output(j - 1, 1 - n % 2)
                        attended(j, n % 2)
                for j in range(ROW_TILES - 3, ROW_TILES):
                    if j + 2 < ROW_TILES:
                        project(j + 2, j % 2)
                    output(j - 1, 1 - j % 2)
                    attended(j, j % 2)
                output(ROW_TILES - 1, 1)

            pe.wait_ge(w_loaded, 16)
            pe.wait_ge(sem("sim_sqr"), 1)
            nc.tensor.matmul(bank(7)[:, 0:E], ones[:, :], simn[:, :], start=True, stop=True).then_inc(sem("sim_sq"), 1)
            for s, stage in enumerate((ffn, recurrence, ffn, experts, heads, experts)[:STAGES]):
                if s == 3:
                    pe.wait_ge(sem("late_loaded"), 16)
                stage(s)

        @block.scalar
        def _(act):
            for s in (0,):
                for name in ("xt_copied", "u_copied", "at_copied", "g2_copied"):
                    act.sem_inc(sem(name, s), HEAD)
            for name in ("tx_done", "ta_done", "aa_done", "m_done"):
                act.sem_inc(sem(name, 1), HEAD)
            for s in (3,):
                for name in ("xt_copied", "ge_done", "qt_hi", "kt_hi", "exp_done", "pt_hi", "ot_copied", "at_copied", "rwt_hi"):
                    act.sem_inc(sem(name, s), HEAD)
                act.sem_inc(sem("prod_done", s), PROD)
            for name in ("xt_copied", "hq_copied", "hw_done", "ot_copied"):
                act.sem_inc(sem(name, 4), HEAD)
            own = Steps(act, sem("act_steps"))

            def pair_loop(pairs, body):
                with act.Fori(0, pairs) as i:
                    for par in range(2):
                        body(2 * i + par, par)

            def setup():
                act.wait_ge(w_loaded, 16)
                act.wait_ge(sem("sp_abs"), 1)
                own.did(nc.scalar.activation(sp_t[:, 1:2], sp_t[:, 0:1], ACT.Exp, scale=-1.0))
                own.settle()
                nc.scalar.activation(sp_t[:, 2:3], sp_t[:, 1:2], ACT.Ln, bias=one_col, scale=1.0).then_inc(sem("sp_ln"), 1)
                nc.scalar.activation(sim_t[:, 1, :], wt["gates"][:, :], ACT.Tanh, scale=0.5).then_inc(sem("gates_tanh"), 1)
                act.wait_ge(sem("sim_sq"), 1)
                nc.scalar.activation(sim_t[:, 0, :], bank(7)[:, 0:E], ACT.Sqrt).then_inc(sem("sim_norm"), 1)

            def norm(s):
                C0, N0 = counted(s)
                act.wait_ge(sem("var_ready", s), REP[s] + 1)
                if s in (3, 5):
                    own.did(nc.scalar.activation(st_b[:, :], st_b[:, :], ACT.Sqrt))
                nc.scalar.activation(var[:, :], var[:, :], ACT.Sqrt).then_inc(sem("sd_ready", s), 1)

            def copy_xt(s, used, width=CHUNK):
                C0 = counted(s)[0]

                def run(c, par):
                    act.wait_ge(sem("xt_done", s), after(C0 + c))
                    act.wait_ge(sem(used, s), free(C0 + c))
                    nc.scalar.activation(xt[:, par, 0:width], bank(par)[:, 0:width], ACT.Copy).then_inc(sem("xt_copied", s), 1)
                return run

            def ffn(s):
                C0, N0 = counted(s)
                norm(s)
                to_xt = copy_xt(s, "u_done")

                def first(c, par):
                    to_xt(c, par)
                    act.wait_ge(sem("u_done", s), after(C0 + c))
                    nc.scalar.activation(big_a[:, bass.ds(CHUNK * c, CHUNK)], bank(4 + par)[:, :], ACT.Identity,
                                         bias=wt["b1"][:, :]).then_inc(sem("u_copied", s), 1)

                pair_loop(CHUNKS // 2, first)
                act.wait_ge(sem("lv_ready", s), REP[s] + 1)
                nc.scalar.activation(st_a[:, :], st_a[:, :], ACT.Sqrt).then_inc(sem("ls_ready", s), 1)
                act.wait_ge(sem("delta_ready", s), REP[s] + 1)
                nc.scalar.activation(e4[:, :, :], e4[:, :, :], ACT.Sqrt).then_inc(sem("root_ready", s), 1)

                def high_weights(c, par):
                    act.wait_ge(sem("at_done", s), after(C0 + c))
                    act.wait_ge(sem("g_done", s), free(C0 + c))
                    nc.scalar.activation(at_r[:, par, :], bank(par)[0:4 * E, :], ACT.Copy).then_inc(sem("at_copied", s), 1)

                def second(c, par, ahead):
                    if ahead:
                        high_weights(c + 1, 1 - par)
                    act.wait_ge(sem("g_done", s), after(C0 + c))
                    nc.scalar.activation(big_b[:, bass.ds(CHUNK * c, CHUNK)], bank(4 + par)[:, :], ACT.Copy).then_inc(sem("g2_copied", s), 1)

                high_weights(0, 0)
                with act.Fori(0, CHUNKS // 2 - 1) as i:
                    for par in range(2):
                        second(2 * i + par, par, True)
                second(CHUNKS - 2, 0, True)
                second(CHUNKS - 1, 1, False)
                act.preload_act_table(ACT.Gelu)
                with act.Fori(0, CHUNKS) as c:
                    for j in range(OC):
                        act.wait_ge(sem("h_done", s), OC * c + (OC * C0 + j + 1))
                        nc.scalar.activation(h_s[:, j, :], bank(j)[:, :], ACT.Gelu).then_inc(sem("gelu_done", s), 1)

            def recurrence(s):
                C0, N0 = counted(s)
                norm(s)
                act.preload_act_table(ACT.Exp)

                def gates(c, par):
                    tok = bass.ds(CHUNK * c, CHUNK)
                    act.wait_ge(sem("gx_done", s), after(C0 + c))
                    act.wait_ge(sem("bx_done", s), free(C0 + c))
                    nc.scalar.activation(tx_s[:, par, :], bank(2 + par)[:, :], ACT.Tanh, scale=0.5).then_inc(sem("tx_done", s), 1)
                    act.wait_ge(sem("ga_done", s), after(C0 + c))
                    act.wait_ge(sem("aa_done", s), free(C0 + c))
                    nc.scalar.activation(ta_s[:, par, :], bank(4 + par)[:, :], ACT.Tanh, scale=0.5).then_inc(sem("ta_done", s), 1)
                    act.wait_ge(sem("ta_done", s), after(C0 + c))
                    nc.scalar.activation(big_a[:, tok], ta_s[:, par, :], ACT.Exp, scale=c1_half[:, :], bias=c1_half[:, :])
                    nc.scalar.activation(big_b[:, tok], ta_s[:, par, :], ACT.Exp, scale=c1[:, :], bias=c1[:, :]).then_inc(sem("aa_done", s), 1)

                act.wait_ge(sem("c1_ready"), 1)
                pair_loop(CHUNKS // 2, gates)
                act.preload_act_table(ACT.Sqrt)
                act.wait_ge(sem("aa_done", s), after(C0 + CHUNKS - 1))

                def roots(c, par):
                    tok = bass.ds(CHUNK * c, CHUNK)
                    nc.scalar.activation(big_b[:, tok], big_b[:, tok], ACT.Sqrt, scale=-1.0, bias=one_col).then_inc(sem("m_done", s), 1)

                pair_loop(CHUNKS // 2, roots)

            def experts(s):
                C0, N0 = counted(s)
                norm(s)
                act.preload_act_table(ACT.Exp)

                def expo(c, par):
                    act.wait_ge(sem("gd_ready", s), after(C0 + c))
                    nc.scalar.activation(ge[:, par], ge[:, par], ACT.Exp).then_inc(sem("ge_done", s), 1)

                def copy(c, par):
                    act.wait_ge(sem("xt_done", s), after(C0 + c))
                    act.wait_ge(sem("y_done", s), YC * c + YC * (C0 + 1))
                    nc.scalar.activation(xt_h[:, par, :], bank(par)[:, :], ACT.Copy).then_inc(sem("xt_copied", s), 1)

                def products(c, par, t):
                    act.wait_ge(sem("qkv_done", s), CT * c + free(N0 + t))
                    for m, g in enumerate(ACT_GROUPS):
                        act.wait_ge(sem("y_done", s), YC * c + ((E // 2) * (N0 + t) + g + 1 + 2 * YC))
                        for h in range(2):
                            e = 2 * g + h
                            nc.scalar.activation(prod[:, t % 2, 2 * m + h, :], bank(4 + g % RING)[:, h * QKV:(h + 1) * QKV], ACT.Copy,
                                                 scale=gate_s[:, par, t, e:e + 1]).then_inc(sem("prod_done", s), 1)

                def main(c, par, ahead):
                    if ahead:
                        copy(c + 1, 1 - par)
                    act.wait_ge(sem("rw_done", s), after(C0 + c))
                    for t in range(CT):
                        products(c, par, t)
                        if ahead and t == 2:
                            expo(c + 1, 1 - par)

                copy(0, 0)
                expo(0, 0)
                with act.Fori(0, CHUNKS // 2 - 1) as i:
                    for par in range(2):
                        main(2 * i + par, par, True)
                main(CHUNKS - 2, 0, True)
                main(CHUNKS - 1, 1, False)
                per_row = T // CHUNK
                with act.Fori(0, B) as b:
                    U0, M0, A0 = (REP[s] * B + b) * len(UNITS), (REP[s] * B + b) * len(TURNS), (REP[s] * B + b) * PAIRS
                    act.wait_ge(sem("qkv_done", s), after(N0 + TILES - 1))
                    nc.scalar.activation(v_s[:, :, 0:HD], qkv[:, bass.ds(ROW_TILES * b, ROW_TILES), 2 * HD:QKV], ACT.Copy).then_inc(sem("v_hi", s), 1)
                    for k in range(per_row):
                        c, par = per_row * b + k, k % 2
                        act.wait_ge(sem("qkt_done", s), after(C0 + c))
                        nc.scalar.activation(q_t[:, k * CHUNK:(k + 1) * CHUNK], bank(par)[:, :], ACT.Copy).then_inc(sem("qt_hi", s), 1)
                        nc.scalar.activation(k_h[:, k * CHUNK:(k + 1) * CHUNK], bank(2 + par)[:, :], ACT.Copy).then_inc(sem("kt_hi", s), 1)

                    def probabilities(u):
                        i, k0, k1 = UNITS[u]
                        if k0 == 0:
                            act.wait_ge(sem("max_ready", s), after(N0 + ROW_TILES * b + i))
                        nc.scalar.activation(prob[:, i % 4, k0 * P:k1 * P], bank(2 * (u % 2), 2)[:, 0:(k1 - k0) * P], ACT.Exp,
                                             scale=HD ** -0.5, bias=neg_max[:, i % 4:i % 4 + 1],
                                             accum_out=row_sum[:, i, k0 // 8:k0 // 8 + 1]).then_inc(sem("exp_done", s), 1)

                    def high_part(m):
                        act.wait_ge(sem("pt_done", s), after(M0 + m))
                        width = P * turn_tiles(m)
                        nc.scalar.activation(pt[m % 3][0][:, 0:width], bank(slot_bank(("turn", m)))[:, 0:width], ACT.Copy).then_inc(sem("pt_hi", s), 1)

                    def halves(a):
                        act.wait_ge(sem("ot_done", s), after(A0 + a))
                        act.wait_ge(sem("at_done", s), free(A0 + a))
                        nc.scalar.activation(o_s[:, a % 2, :], bank(6)[:, 0:2 * P], ACT.Copy).then_inc(sem("ot_copied", s), 1)

                    def attention(a):
                        act.wait_ge(sem("at_done", s), after(A0 + a))
                        nc.scalar.activation(att_t[:, a * 2 * P:(a + 1) * 2 * P], bank(slot_bank(("fold", a)))[:, 0:2 * P], ACT.Copy)\
                            .then_inc(sem("at_copied", s), 1)

                    due, turns = [], 0
                    for kind, n in ORDER:
                        if kind == "scores":
                            if UNITS[n][1] == 0:
                                for u in due:
                                    probabilities(u)
                                due, turns = [], 0
                            due.append(n)
                        if kind == "turn":
                            if TURNS[n][1] == 0 and last_unit(2 * TURNS[n][0] + 1) in due:
                                for u in due:
                                    probabilities(u)
                                due = []
                            high_part(n)
                            turns += 1
                            if turns >= EXP_DELAY and due:
                                probabilities(due.pop(0))
                        if kind == "fold":
                            attention(n)
                        if kind == "mix" and TURNS[n][0] == TURNS[n][1]:
                            halves(TURNS[n][0])

                    for k in range(per_row):
                        c, par = per_row * b + k, k % 2
                        act.wait_ge(sem("rwt_done", s), after(C0 + c))
                        act.wait_ge(sem("bc_done", s), (E // 2) * (C0 + per_row * b) + (E // 2) * max(k, 1))
                        nc.scalar.activation(rw_t[:, par, :], bank(par)[0:4 * E, :], ACT.Copy).then_inc(sem("rwt_hi", s), 1)

            def heads(s):
                C0, N0 = counted(s)
                norm(s)
                act.preload_act_table(ACT.Exp)

                def to_xt(j, par):
                    act.wait_ge(sem("xt_done", s), after(C0 + j))
                    act.wait_ge(sem("hq_done", s), free(C0 + j))
                    nc.scalar.activation(xt[:, par, 0:2 * P], bank(0)[:, 0:2 * P], ACT.Copy).then_inc(sem("xt_copied", s), 1)

                def copy_qkv(j, par):
                    act.wait_ge(sem("hq_done", s), after(C0 + j))
                    act.wait_ge(sem("ho_ready", s), free(C0 + j))
                    nc.scalar.activation(hq[:, par], bank(2 + 2 * par, 2).rearrange("p (t e) -> p t e", t=2)[:, :, 0:3 * D], ACT.Copy).then_inc(sem("hq_copied", s), 1)

                def weights(j, par):
                    act.wait_ge(sem("hd_ready", s), after(C0 + j))
                    nc.scalar.activation(hw[:, par], hw[:, par], ACT.Exp).then_inc(sem("hw_done", s), 1)

                def copy_attended(j, par):
                    act.wait_ge(sem("ot_done", s), after(C0 + j))
                    act.wait_ge(sem("out_done", s), free(C0 + j))
                    nc.scalar.activation(ot_s[:, par], bank(1)[:, 0:2 * P].rearrange("p (t d) -> p t d", t=2), ACT.Copy).then_inc(sem("ot_copied", s), 1)

                to_xt(0, 0)
                to_xt(1, 1)
                copy_qkv(0, 0)
                to_xt(2, 0)
                copy_qkv(1, 1)
                weights(0, 0)
                to_xt(3, 1)
                weights(1, 1)
                copy_qkv(2, 0)
                copy_attended(0, 0)
                with act.Fori(0, ROW_TILES // 2 - 2) as i:
                    for n in (1, 2):
                        j = 2 * i + n
                        to_xt(j + 3, 1 - n % 2)
                        weights(j + 1, 1 - n % 2)
                        copy_qkv(j + 2, n % 2)
                        copy_attended(j, n % 2)
                for j in range(ROW_TILES - 3, ROW_TILES):
                    if j + 1 < ROW_TILES:
                        weights(j + 1, 1 - j % 2)
                    if j + 2 < ROW_TILES:
                        copy_qkv(j + 2, j % 2)
                    copy_attended(j, j % 2)

            setup()
            for s, stage in enumerate((ffn, recurrence, ffn, experts, heads, experts)[:STAGES]):
                stage(s)

        @block.vector
        def _(dve):
            v = nc.vector
            for s in (0,):
                for name in ("lg_copied", "at_lo", "z1_done", "z2_ready", "x_added"):
                    dve.sem_inc(sem(name, s), HEAD)
            for name in ("xt_copied", "bx_done", "y_ready", "x_added"):
                dve.sem_inc(sem(name, 1), HEAD)
            for s in (3,):
                for name in ("lg_copied", "gd_ready", "rw_done", "xt_lo", "qk_ready", "qt_lo", "kt_lo", "max_ready", "pt_lo", "rwt_lo", "x_added"):
                    dve.sem_inc(sem(name, s), HEAD)
                dve.sem_inc(sem("acc_done", s), ACC)
                dve.sem_inc(sem("mx_done", s), E // 2)
            for name in ("hd_ready", "hv_ready", "ho_ready", "x_added"):
                dve.sem_inc(sem(name, 4), HEAD)
            own = Steps(dve, sem("dve_steps"))

            def then(instruction):
                own.did(instruction)
                own.settle()

            def pair_loop(pairs, per, body):
                with own.loop(0, pairs, 2 * per) as i:
                    for par in range(2):
                        body(2 * i + par, par)

            def setup():
                dve.wait_ge(w_loaded, 16)
                a = wt["a_param"]
                then(v.tensor_scalar(sp_t[:, 3:4], a[:, :], -1.0, None, ALU.mult))
                v.tensor_tensor(sp_t[:, 0:1], a[:, :], sp_t[:, 3:4], ALU.max).then_inc(sem("sp_abs"), 1)
                dve.wait_ge(sem("sp_ln"), 1)
                then(v.scalar_tensor_tensor(sp_t[:, 3:4], a[:, :], 0.0, sp_t[:, 2:3], ALU.max, ALU.add))
                own.did(v.tensor_scalar(c1_half[:, :], sp_t[:, 3:4], -0.5 * LRU_C, None, ALU.mult))
                v.tensor_scalar(c1[:, :], sp_t[:, 3:4], -LRU_C, None, ALU.mult).then_inc(sem("c1_ready"), 1)
                dve.wait_ge(sem("gates_tanh"), 1)
                own.did(v.tensor_scalar(sgate[:, :], sim_t[:, 1, :], 0.5, 0.5, ALU.mult, ALU.add))
                v.tensor_tensor(simn[:, :], wt["sim"][:, :], wt["sim"][:, :], ALU.mult).then_inc(sem("sim_sqr"), 1)
                dve.wait_ge(sem("sim_norm"), 1)
                then(v.tensor_scalar(sim_t[:, 0, :], sim_t[:, 0, :], 1e-12, None, ALU.max))
                then(v.reciprocal(sim_t[:, 0, :], sim_t[:, 0, :]))
                then(v.tensor_tensor(simn[:, :], wt["sim"][:, :], sim_t[:, 0, :], ALU.mult))
                then(v.tensor_copy(sim_h[:, :], simn[:, :]))
                own.did(v.tensor_copy(ident_b[:, :], ident))
                own.did(v.tensor_copy(causal_b[:, :], causal))
                v.tensor_tensor(sim_l[:, :], simn[:, :], sim_h[:, :].bitcast(F32), ALU.subtract).then_inc(sem("sim_ready"), 1)

            def split_weights():
                dve.wait_ge(sem("split_loaded"), 16)
                own.did(v.tensor_copy(wo1_h[:, :], wt["wo1"]))
                own.did(v.tensor_copy(win2_r[:, :, 0:R], wt["win2"]))
                then(v.tensor_copy(pick[:, :, :], wt["pick"].rearrange("p (g n) -> p g n", n=P)))
                own.did(v.tensor_tensor(win2_r[:, :, R:2 * R], wt["win2"], win2_r[:, :, 0:R].bitcast(F32), ALU.subtract))
                own.did(v.tensor_tensor(wo1_l[:, :], wt["wo1"], wo1_h[:, :].bitcast(F32), ALU.subtract))

            def norm(s):
                C0, N0 = counted(s)
                own.settle()
                m_even, m_odd = stats[:, :, 1], stats[:, :, 4]
                own.did(v.tensor_tensor(mean[:, :], m_even, m_odd, ALU.add))
                own.did(v.tensor_tensor(st_a[:, :], m_even, m_odd, ALU.subtract))
                then(v.tensor_tensor(st_b[:, :], stats[:, :, 2], stats[:, :, 5], ALU.add))
                own.did(v.tensor_scalar(mean[:, :], mean[:, :], 0.5, None, ALU.mult))
                then(v.scalar_tensor_tensor(st_a[:, :], st_a[:, :], 0.25, st_a[:, :], ALU.mult, ALU.mult))
                then(v.scalar_tensor_tensor(st_a[:, :], st_b[:, :], 1.0 / D, st_a[:, :], ALU.mult, ALU.add))
                if s in (3, 5):
                    own.did(v.tensor_scalar(st_b[:, :], st_a[:, :], float(D), None, ALU.mult))
                v.tensor_scalar(var[:, :], st_a[:, :], LN_EPS, None, ALU.add).then_inc(sem("var_ready", s), 1)
                dve.wait_ge(sem("sd_ready", s), REP[s] + 1)
                v.reciprocal(rstd[:, :], var[:, :]).then_inc(sem("norm_ready", s), 1)
                if s in (3, 5):
                    dve.wait_ge(sem("norm_ready", s), REP[s] + 1)
                    then(v.tensor_tensor(st_b[:, :], st_b[:, :], rstd[:, :], ALU.mult))
                    then(v.tensor_scalar(st_b[:, :], st_b[:, :], 1e-12, None, ALU.max))
                    then(v.reciprocal(inv_norm[:, :], st_b[:, :]))

            def add_to_x(s, c, par, source, scale, tiles=CT):
                C0 = counted(s)[0]
                part = X[:, bass.ds(tiles * c, tiles), :].rearrange("p t d -> p (t d)")
                v.scalar_tensor_tensor(part, source, scale, part, ALU.mult, ALU.add).then_inc(sem("x_added", s), 1)
                dve.wait_ge(sem("x_added", s), after(C0 + c))
                for t in range(tiles):
                    own.did(v.bn_stats(stats[:, bass.ds(tiles * c + t, 1), :].rearrange("p o k -> p (o k)"),
                                       X[:, bass.ds(tiles * c + t, 1), :].rearrange("p o d -> p (o d)")))

            def ffn(s):
                C0, N0 = counted(s)
                then(v.tensor_copy(cc_h[:, :], wt["c12"]))
                v.tensor_tensor(cc_l[:, :], wt["c12"], cc_h[:, :].bitcast(F32), ALU.subtract).then_inc(sem("cc_ready", s), 1)
                norm(s)

                def sort(c, par):
                    some = slice(0, CT * E)
                    dve.wait_ge(sem("lg_done", s), after(C0 + c))
                    own.did(v.tensor_copy(lg[:, bass.ds(CT * c, CT), :], bank(2 + par)[:, some].rearrange("p (t e) -> p t e", t=CT)))
                    for t in range(CT):
                        own.did(v.max(srt_s[:, par, t, 0:8], bank(2 + par)[:, t * E:(t + 1) * E]))
                    own.settle()
                    carry_wait(dve)
                    for t in range(CT):
                        last = v.match_replace(rest_s[:, t, :], srt_s[:, par, t, 0:8], bank(2 + par)[:, t * E:(t + 1) * E], -3e38)
                    last.then_inc(sem("lg_copied", s), 1)
                    dve.wait_ge(sem("lg_copied", s), after(C0 + c))
                    carry_wait(dve)
                    for t in range(CT):
                        own.did(v.max(srt_s[:, par, t, 8:16], rest_s[:, t, :]))
                    own.settle()
                    own.did(v.tensor_copy(srt[:, bass.ds(CT * c, CT), :], srt_s[:, par]))
                    own.settle()

                pair_loop(CHUNKS // 2, 10, sort)

                flat = "p t e -> p (t e)"
                ks = k_row[:, :].unsqueeze(1).broadcast_to([P, TILES, E])
                iks = inv_k[:, :].unsqueeze(1).broadcast_to([P, TILES, E])
                then(v.reduce_sum(mean[:, :], lg[:, :, :], AX.X))
                then(v.tensor_scalar(mean[:, :], mean[:, :], 1.0 / E, None, ALU.mult))
                own.did(v.tensor_tensor(srt[:, :, :], srt[:, :, :], over_e(mean[:, :]), ALU.subtract))
                then(v.tensor_tensor(lg[:, :, :], lg[:, :, :], over_e(mean[:, :]), ALU.subtract))
                then(v.tensor_tensor(e1[:, :, :], lg[:, :, :], lg[:, :, :], ALU.mult))
                then(v.reduce_sum(st_a[:, :], e1[:, :, :], AX.X))
                v.tensor_scalar(st_a[:, :], st_a[:, :], 1.0 / E, LN_EPS, ALU.mult, ALU.add).then_inc(sem("lv_ready", s), 1)
                dve.wait_ge(sem("ls_ready", s), REP[s] + 1)
                then(v.reciprocal(st_a[:, :], st_a[:, :]))
                then(v.tensor_scalar(st_a[:, :], st_a[:, :], 0.5, None, ALU.mult))
                own.did(v.tensor_tensor(srt[:, :, :], srt[:, :, :], over_e(st_a[:, :]), ALU.mult))
                then(v.tensor_tensor(lg[:, :, :], lg[:, :, :], over_e(st_a[:, :]), ALU.mult))
                own.did(v.tensor_copy(st_b[:, :], srt[:, :, 0]))
                own.settle()
                own.did(v.tensor_tensor(lg[:, :, :], lg[:, :, :], over_e(st_b[:, :]), ALU.subtract))
                then(v.tensor_tensor(srt[:, :, :], srt[:, :, :], over_e(st_b[:, :]), ALU.subtract))
                own.did(v.tensor_tensor_scan(e1[:, :, :].rearrange(flat), seg[:, :], srt[:, :, :].rearrange(flat), 0.0, ALU.mult, ALU.add))
                then(v.tensor_tensor(e2[:, :, :], srt[:, :, :], srt[:, :, :], ALU.mult))
                own.did(v.tensor_tensor(e1[:, :, :], e1[:, :, :], iks, ALU.mult))
                then(v.tensor_tensor_scan(e3[:, :, :].rearrange(flat), seg[:, :], e2[:, :, :].rearrange(flat), 0.0, ALU.mult, ALU.add))
                own.did(v.tensor_tensor(e3[:, :, :], e3[:, :, :], iks, ALU.mult))
                then(v.tensor_tensor(e4[:, :, :], e1[:, :, :], e1[:, :, :], ALU.mult))
                then(v.tensor_tensor(e4[:, :, :], e3[:, :, :], e4[:, :, :], ALU.subtract))
                then(v.tensor_tensor(e4[:, :, :], e4[:, :, :], ks, ALU.mult))
                then(v.tensor_scalar(e4[:, :, :], e4[:, :, :], -1.0, 1.0, ALU.mult, ALU.add))
                then(v.tensor_tensor(e4[:, :, :], e4[:, :, :], iks, ALU.mult))
                v.tensor_scalar(e4[:, :, :], e4[:, :, :], 0.0, None, ALU.max).then_inc(sem("delta_ready", s), 1)
                dve.wait_ge(sem("root_ready", s), REP[s] + 1)
                then(v.tensor_tensor(e1[:, :, :], e1[:, :, :], e4[:, :, :], ALU.subtract))
                then(v.tensor_tensor(e2[:, :, :], e1[:, :, :], srt[:, :, :], ALU.is_le))
                then(v.reduce_sum(st_a[:, :], e2[:, :, :], AX.X))
                then(v.tensor_tensor(e2[:, :, :], ks, over_e(st_a[:, :]), ALU.is_equal))
                then(v.tensor_tensor(e2[:, :, :], e2[:, :, :], e1[:, :, :], ALU.mult))
                then(v.reduce_sum(st_b[:, :], e2[:, :, :], AX.X))
                then(v.tensor_tensor(lg[:, :, :], lg[:, :, :], over_e(st_b[:, :]), ALU.subtract))
                then(v.tensor_scalar(lg[:, :, :], lg[:, :, :], 0.0, None, ALU.max))
                v.tensor_tensor(gate[:, :, :], lg[:, :, :], lg[:, :, :], ALU.mult).then_inc(sem("entmax_done", s), 1)

                def first(c, par):
                    tok = bass.ds(CHUNK * c, CHUNK)
                    dve.wait_ge(sem("g_done", s), after(C0 + c))
                    then(v.tensor_tensor(z1_s[:, par, :], bank(2 + par)[:, :], big_a[:, tok], ALU.mult))
                    then(v.tensor_copy(z1_r[:, tok], z1_s[:, par, :]))
                    v.tensor_tensor(z1_r[R:P, tok], z1_s[R:P, par, :], z1_r[R:P, tok].bitcast(F32), ALU.subtract).then_inc(sem("z1_done", s), 1)

                dve.wait_ge(sem("u_copied", s), after(C0 + CHUNKS - 1))


                def low_weights(c, par):
                    dve.wait_ge(sem("at_copied", s), after(C0 + c))
                    v.tensor_tensor(at_r[2 * E:4 * E, par, :], bank(par)[2 * E:4 * E, :], at_r[2 * E:4 * E, par, :].bitcast(F32),
                                    ALU.subtract).then_inc(sem("at_lo", s), 1)

                low_weights(0, 0)
                with own.loop(0, CHUNKS // 2 - 1, 4) as i:
                    for par in range(2):
                        low_weights(2 * i + par + 1, 1 - par)
                        first(2 * i + par, par)
                low_weights(CHUNKS - 1, 1)
                first(CHUNKS - 2, 0)
                first(CHUNKS - 1, 1)
                dve.wait_ge(sem("g2_copied", s), after(C0 + CHUNKS - 1))

                def high_part(c, j):
                    dve.wait_ge(sem("gelu_done", s), OC * c + (OC * C0 + j + 1))
                    v.tensor_copy(h_h[:, j, :], h_s[:, j, :]).then_inc(sem("h_hi", s), 1)
                    if j == OC - 1:
                        dve.wait_ge(sem("h_hi", s), OC * c + OC * (C0 + 1))
                        v.tensor_tensor(h_l[:, j, :], h_s[:, j, :], h_h[:, j, :].bitcast(F32), ALU.subtract).then_inc(sem("h_lo_last", s), 1)

                def second(c, par):
                    dve.wait_ge(sem("z2_done", s), after(C0 + c))
                    dve.wait_ge(sem("out_done", s), free(C0 + c))
                    v.scalar_tensor_tensor(z2_s[:, par, :], bank(4 + par)[:, :], wt["b2"][:, :],
                                           big_b[:, bass.ds(CHUNK * c, CHUNK)], ALU.add, ALU.mult).then_inc(sem("z2_ready", s), 1)

                def add(c, par):
                    dve.wait_ge(sem("out_done", s), after(C0 + c))
                    add_to_x(s, c, par, bank(6 + par), 0.5)

                def chunk(c, par, behind):
                    for j in range(OC):
                        high_part(c + 1, j)
                        if behind and j == 1:
                            add(c - 1, 1 - par)
                    second(c, par)

                for j in range(OC):
                    high_part(0, j)
                chunk(0, 0, False)
                with own.loop(0, CHUNKS // 2 - 1, 2 * CT) as i:
                    for n in (1, 2):
                        chunk(2 * i + n, n % 2, True)
                add(CHUNKS - 2, 0)
                second(CHUNKS - 1, 1)
                add(CHUNKS - 1, 1)

            def recurrence(s):
                C0, N0 = counted(s)
                norm(s)

                def gates(c, par):
                    dve.wait_ge(sem("xt_done", s), after(C0 + c))
                    dve.wait_ge(sem("ga_done", s), free(C0 + c))
                    v.tensor_copy(xt[:, par, :], bank(par)).then_inc(sem("xt_copied", s), 1)
                    dve.wait_ge(sem("tx_done", s), after(C0 + c))
                    dve.wait_ge(sem("xt_copied", s), after(C0 + c))
                    v.scalar_tensor_tensor(big_c[:, bass.ds(CHUNK * c, CHUNK)], tx_s[:, par, :], 1.0, xt[:, par, :],
                                           ALU.add, ALU.mult).then_inc(sem("bx_done", s), 1)

                pair_loop(CHUNKS // 2, 0, gates)
                dve.wait_ge(sem("bx_done", s), after(C0 + CHUNKS - 1))
                per_row = T // CHUNK

                with own.loop(0, B, per_row * (1 + CT)) as b:
                    def recur(k):
                        c, par = per_row * b + k, k % 2
                        tok = bass.ds(CHUNK * c, CHUNK)
                        dve.wait_ge(sem("m_done", s), after(C0 + c))
                        then(v.scalar_tensor_tensor(big_c[:, tok], big_c[:, tok], 0.5, big_b[:, tok], ALU.mult, ALU.mult))
                        dve.wait_ge(sem("y_ready", s), after(C0 + c - 1))
                        dve.wait_ge(sem("yt_done", s), free(C0 + c))
                        v.tensor_tensor_scan(y_s[:, par, :], big_a[:, tok], big_c[:, tok],
                                             0.0 if k == 0 else y_s[:, 1 - par, CHUNK - 1:CHUNK],
                                             ALU.mult, ALU.add).then_inc(sem("y_ready", s), 1)

                    def add(k):
                        dve.wait_ge(sem("yt_done", s), after(C0 + per_row * b + k))
                        add_to_x(s, per_row * b + k, k % 2, bank(6 + k % 2), 1.0)

                    for k in range(per_row):
                        recur(k)
                        if k:
                            add(k - 1)
                    add(per_row - 1)

            def experts(s):
                C0, N0 = counted(s)
                norm(s)
                some = slice(0, CT * E)
                flat = "p t e -> p (t e)"

                def route(c, par, step):
                    t1, t2 = m8[:, par, :, 0], m8[:, par, :, 1]
                    own.settle()
                    if step == 0:
                        dve.wait_ge(sem("lg_done", s), after(C0 + c))
                        v.tensor_tensor(gl[:, :, :], bank(2 + par)[:, some].rearrange("p (t e) -> p t e", t=CT),
                                        inv_norm[:, bass.ds(CT * c, CT)].unsqueeze(2).broadcast_to([P, CT, E]),
                                        ALU.mult).then_inc(sem("lg_copied", s), 1)
                    elif step == 1:
                        dve.wait_ge(sem("lg_copied", s), after(C0 + c))
                        own.did(v.tensor_tensor(gl[:, :, :], gl[:, :, :], sgate[:, :].unsqueeze(1).broadcast_to([P, CT, E]), ALU.subtract))
                    elif step == 2:
                        carry_wait(dve)
                        for t in range(CT):
                            own.did(v.max(m8[:, par, t, :], gl[:, t, :]))
                    elif step == 3:
                        own.did(v.tensor_scalar(gc[:, 0, :], t1, 0.0, None, ALU.max))
                        own.did(v.tensor_scalar(g1[:, :, :], gl[:, :, :], 0.0, None, ALU.max))
                        own.did(v.tensor_tensor(gc[:, 1, :], t1, t2, ALU.is_equal))
                        own.did(v.tensor_scalar(gc[:, 2, :], t1, 0.0, None, ALU.is_le))
                        own.did(v.tensor_tensor(g3[:, :, :], gl[:, :, :], over_e(t2), ALU.is_equal))
                    elif step == 4:
                        v.tensor_tensor(ge[:, par], g1[:, :, :], over_e(gc[:, 0, :]), ALU.subtract).then_inc(sem("gd_ready", s), 1)
                        own.did(v.tensor_scalar(gc[:, 1, :], gc[:, 1, :], 1.0, None, ALU.add))
                        own.did(v.tensor_tensor(g2[:, :, :], gl[:, :, :], over_e(t2), ALU.is_gt))
                        own.did(v.tensor_tensor_scan(g4[:, :, :].rearrange(flat), seg[:, some], g3[:, :, :].rearrange(flat), 0.0, ALU.mult, ALU.add))
                    elif step == 5:
                        own.did(v.tensor_tensor(g4[:, :, :], g4[:, :, :], over_e(gc[:, 1, :]), ALU.is_le))
                    elif step == 6:
                        own.did(v.tensor_tensor(g3[:, :, :], g3[:, :, :], g4[:, :, :], ALU.mult))
                    elif step == 7:
                        own.did(v.tensor_tensor(g3[:, :, :], g3[:, :, :], g2[:, :, :], ALU.add))
                    elif step == 8:
                        own.did(v.tensor_tensor(g3[:, :, :], g3[:, :, :], over_e(gc[:, 2, :]), ALU.mult))
                    elif step == 9:
                        own.did(v.scalar_tensor_tensor(g3[:, :, :], gl[:, :, :], 0.0, g3[:, :, :], ALU.is_gt, ALU.add))
                    elif step == 10:
                        dve.wait_ge(sem("ge_done", s), after(C0 + c))
                        own.did(v.tensor_tensor(g3[:, :, :], g3[:, :, :], ge[:, par], ALU.mult))
                    elif step == 11:
                        own.did(v.reduce_sum(gc[:, 3, :], g3[:, :, :], AX.X))
                    elif step == 12:
                        own.did(v.reciprocal(gc[:, 3, :], gc[:, 3, :]))
                    elif step == 13:
                        v.tensor_tensor(gate_s[:, par], g3[:, :, :], over_e(gc[:, 3, :]), ALU.mult).then_inc(sem("rw_done", s), 1)
                    elif step == 14:
                        dve.wait_ge(sem("rw_done", s), after(C0 + c))
                        own.did(v.tensor_copy(gate[:, bass.ds(CT * c, CT), :], gate_s[:, par]))

                ROUTE_STEPS = 15
                ROUTE = 1 + CT + 5 + 3 + 5 + 3 + 1

                def combine(c, par, t, between=None):
                    q = t % 2
                    dve.wait_ge(sem("qkv_done", s), CT * c + free(N0 + t))
                    for m, g in enumerate(DVE_GROUPS):
                        dve.wait_ge(sem("y_done", s), YC * c + ((E // 2) * (N0 + t) + g + 1 + 2 * YC))
                        for h in range(2):
                            e = 2 * g + h
                            y = bank(4 + g % RING)[:, h * QKV:(h + 1) * QKV]
                            weight = gate_s[:, par, t, e:e + 1]
                            if m == 0:
                                dve.wait_ge(sem("prod_done", s), PROD * CT * c + (PROD * (N0 + t) + PROD + h + 1))
                                last = v.scalar_tensor_tensor(acc[:, q, h, :], y, weight, prod[:, q, h, :], ALU.mult, ALU.add)
                            else:
                                dve.wait_ge(sem("acc_done", s), ACC * CT * c + (ACC * (N0 + t) + ACC + 2 * m - 1 + h))
                                last = v.scalar_tensor_tensor(acc[:, q, h, :], y, weight, acc[:, q, h, :], ALU.mult, ALU.add)
                            last.then_inc(sem("acc_done", s), 1)
                        if between:
                            between(m)

                def low_part(c, par):
                    dve.wait_ge(sem("xt_copied", s), after(C0 + c))
                    v.tensor_tensor(xt_l[:, par, :], bank(par)[:, :], xt_h[:, par, :].bitcast(F32), ALU.subtract).then_inc(sem("xt_lo", s), 1)

                def main(c, par, ahead):
                    groups = len(DVE_GROUPS)
                    for t in range(CT):
                        def between(m):
                            if t == 0 and m == 0:
                                low_part(c + 1, 1 - par)
                            if t > 0:
                                for step in range(ROUTE_STEPS):
                                    if step * (CT - 1) * groups // ROUTE_STEPS == (t - 1) * groups + m:
                                        route(c + 1, 1 - par, step)
                        combine(c, par, t, between if ahead else None)

                dve.wait_ge(sem("sim_ready"), 1)
                low_part(0, 0)
                for step in range(ROUTE_STEPS):
                    route(0, 0, step)
                with own.loop(0, CHUNKS // 2 - 1, 2 * ROUTE) as i:
                    for par in range(2):
                        main(2 * i + par, par, True)
                main(CHUNKS - 2, 0, True)
                main(CHUNKS - 1, 1, False)
                per_row = T // CHUNK

                with own.loop(0, B, len(UNITS) + 2 + CHUNKS // 2 * CT) as b:
                    M0 = (REP[s] * B + b) * len(TURNS)
                    U0 = (REP[s] * B + b) * len(UNITS)
                    def twice(k):
                        c, par = per_row * b + k, k % 2
                        dve.wait_ge(sem("qkt_done", s), free(C0 + c))
                        for copy in range(2):
                            last = v.tensor_copy(qk_s[:, par, :, :, copy, :],
                                                 qkv[:, bass.ds(CT * c, CT), 0:2 * HD].rearrange("p t (m d) -> p t m d", m=2))
                        last.then_inc(sem("qk_ready", s), 1)

                    def low_parts(k):
                        c, par = per_row * b + k, k % 2
                        cols = slice(k * CHUNK, (k + 1) * CHUNK)
                        dve.wait_ge(sem("qt_hi", s), after(C0 + c))
                        v.tensor_tensor(q_t[HD:P, cols], bank(par)[HD:P, :], q_t[HD:P, cols].bitcast(F32), ALU.subtract).then_inc(sem("qt_lo", s), 1)
                        dve.wait_ge(sem("kt_hi", s), after(C0 + c))
                        v.tensor_tensor(k_l[:, cols], bank(2 + par)[:, :], k_h[:, cols].bitcast(F32), ALU.subtract).then_inc(sem("kt_lo", s), 1)

                    dve.wait_ge(sem("qkv_done", s), after(N0 + TILES - 1))
                    twice(0)
                    for k in range(per_row):
                        if k + 1 < per_row:
                            twice(k + 1)
                        low_parts(k)
                    dve.wait_ge(sem("v_hi", s), REP[s] * B + b + 1)
                    v.tensor_tensor(v_s[:, :, HD:2 * HD], qkv[:, bass.ds(ROW_TILES * b, ROW_TILES), 2 * HD:QKV], v_s[:, :, 0:HD].bitcast(F32),
                                    ALU.subtract).then_inc(sem("v_lo", s), 1)

                    def unit_maximum(u):
                        dve.wait_ge(sem("s_done", s), after(U0 + u))
                        i, k0, k1 = UNITS[u]
                        own.did(v.tensor_reduce(row_max[:, u % 4:u % 4 + 1], bank(2 * (u % 2), 2)[:, 0:(k1 - k0) * P], AX.X, ALU.max))
                        if u == last_unit(i):
                            own.settle()
                            neg = neg_max[:, i % 4:i % 4 + 1]
                            maxima = [row_max[:, w % 4:w % 4 + 1] for w, unit in enumerate(UNITS) if unit[0] == i]
                            if len(maxima) == 1:
                                last = v.tensor_scalar(neg, maxima[0], -(HD ** -0.5), None, ALU.mult)
                            else:
                                last = v.tensor_scalar(neg, maxima[0], maxima[1], -(HD ** -0.5), ALU.max, ALU.mult)
                            last.then_inc(sem("max_ready", s), 1)

                    def low_turn(m):
                        width = P * turn_tiles(m)
                        dve.wait_ge(sem("pt_hi", s), after(M0 + m))
                        v.tensor_tensor(pt[m % 3][1][:, 0:width], bank(slot_bank(("turn", m)))[:, 0:width], pt[m % 3][0][:, 0:width].bitcast(F32),
                                        ALU.subtract).then_inc(sem("pt_lo", s), 1)

                    for kind, n in ORDER:
                        if kind == "scores":
                            unit_maximum(n)
                        if kind == "turn":
                            low_turn(n)

                    dve.wait_ge(sem("exp_done", s), after(U0 + len(UNITS) - 1))
                    then(v.tensor_tensor(inv_sum[:, :], row_sum[:, :, 0], row_sum[:, :, 1], ALU.add))
                    then(v.reciprocal(inv_sum[:, :], inv_sum[:, :]))
                    mine = gate[:, bass.ds(ROW_TILES * b, ROW_TILES), :]
                    v.tensor_tensor(mine, mine, inv_sum[:, :].unsqueeze(2).broadcast_to([P, ROW_TILES, E]), ALU.mult).then_inc(sem("rw_scaled", s), 1)

                    def weights(k):
                        c, par = per_row * b + k, k % 2
                        dve.wait_ge(sem("rwt_hi", s), after(C0 + c))
                        v.tensor_tensor(rw_t[2 * E:4 * E, par, :], bank(par)[2 * E:4 * E, :], rw_t[2 * E:4 * E, par, :].bitcast(F32),
                                        ALU.subtract).then_inc(sem("rwt_lo", s), 1)

                    def add(k):
                        dve.wait_ge(sem("og_done", s), (E // 2) * (C0 + per_row * b) + (E // 2) * (k + 2))
                        add_to_x(s, per_row * b + k, k % 2, bank(6 + k % 2), 0.5)

                    weights(0)
                    dve.wait_ge(sem("at_copied", s), after((REP[s] * B + b) * PAIRS + PAIRS - 1))
                    for k in range(per_row):
                        n = (E // 2) * (C0 + per_row * b)
                        for g in range(E // 2):
                            dve.wait_ge(sem("bc_done", s), n + ((E // 2) * (k + 1) + g + 1))
                            dve.wait_ge(sem("og_done", s), n + ((E // 2) * (k + 1) + g + 1 - RING))
                            v.tensor_tensor(mx_s[:, g % RING, :], bank(2 + g % RING)[:, :], att_t[:, k * CHUNK:(k + 1) * CHUNK],
                                            ALU.mult).then_inc(sem("mx_done", s), 1)
                            if g == 2 and k:
                                add(k - 1)
                            if g == 4 and k + 1 < per_row:
                                weights(k + 1)
                    add(per_row - 1)

            def heads(s):
                C0, N0 = counted(s)
                own.did(v.tensor_copy(hb[:, :], wt["b_qkv"]))
                own.did(v.tensor_copy(h_one[:, :], wt["fold"][:, 0:1].broadcast_to([P, P])))
                own.settle()
                v.tensor_tensor(hb[HD:P, :], wt["b_qkv"][HD:P, :], hb[HD:P, :].bitcast(F32), ALU.subtract).then_inc(sem("hb_ready"), 1)
                norm(s)
                scaling = (D // HEADS) ** -0.5
                hd = D // HEADS

                def scores(j, par):
                    dve.wait_ge(sem("hq_copied", s), after(C0 + j))
                    q, k = hq[:, par, :, 0:D], hq[:, par, :, D:2 * D]
                    then(v.tensor_tensor(hp[:, 2, 0, :], k[:, 0, :], k[:, 1, :], ALU.subtract))
                    then(v.tensor_tensor(hp[:, 0], q, hp[:, 2, 0, :].unsqueeze(1).broadcast_to([P, 2, D]), ALU.mult))
                    then(v.reduce_sum(hr[:, 0], hp[:, 0].rearrange("p t (h d) -> p t h d", h=HEADS), AX.X))
                    own.did(v.tensor_scalar(hw[:, par, 0], hr[:, 0], scaling, 0.0, ALU.mult, ALU.min))
                    v.tensor_scalar(hw[:, par, 1], hr[:, 0], -scaling, 0.0, ALU.mult, ALU.min).then_inc(sem("hd_ready", s), 1)

                def attend(j, par):
                    dve.wait_ge(sem("hw_done", s), after(C0 + j))
                    then(v.tensor_tensor(hr[:, 1], hw[:, par, 0], hw[:, par, 1], ALU.add))
                    then(v.reciprocal(hr[:, 1], hr[:, 1]))
                    v.tensor_tensor(hw[:, par], hw[:, par], hr[:, 1].unsqueeze(1).broadcast_to([P, 2, 2, HEADS]), ALU.mult).then_inc(sem("hv_ready", s), 1)
                    dve.wait_ge(sem("hv_ready", s), after(C0 + j))
                    value = hq[:, par, 0, 2 * D:3 * D].rearrange("p (h d) -> p h d", h=HEADS).unsqueeze(1)
                    then(v.tensor_tensor(hp[:, 0].rearrange("p t (h d) -> p t h d", h=HEADS), value.broadcast_to([P, 2, HEADS, hd]),
                                         hw[:, par, 0].unsqueeze(3).broadcast_to([P, 2, HEADS, hd]), ALU.mult))
                    dve.wait_ge(sem("hv_done", s), after(C0 + j))
                    dve.wait_ge(sem("ot_done", s), free(C0 + j))
                    v.tensor_tensor(ho[:, par], hp[:, 0], hp[:, 1], ALU.add).then_inc(sem("ho_ready", s), 1)

                def put_out(j, par):
                    dve.wait_ge(sem("out_done", s), after(C0 + j))
                    dve.wait_ge(sem("x_biased", s), after(C0 + j))
                    part = X_rows[:, :, bass.ds(j, 1), :].rearrange("p b o d -> p b (o d)")
                    v.tensor_tensor(part, bank(6 + par)[:, 0:2 * D].rearrange("p (t d) -> p t d", t=2), part,
                                    ALU.add).then_inc(sem("x_added", s), 1)
                    dve.wait_ge(sem("x_added", s), after(C0 + j))
                    for r in range(B):
                        own.did(v.bn_stats(stats[:, bass.ds(ROW_TILES * r + j, 1), :].rearrange("p o k -> p (o k)"),
                                           X[:, bass.ds(ROW_TILES * r + j, 1), :].rearrange("p o d -> p (o d)")))

                scores(0, 0)
                scores(1, 1)
                attend(0, 0)
                with own.loop(0, ROW_TILES // 2 - 1, 2 * (4 + 3 + B)) as i:
                    for n in (1, 2):
                        j = 2 * i + n
                        scores(j + 1, 1 - n % 2)
                        attend(j, n % 2)
                        put_out(j - 1, 1 - n % 2)
                attend(ROW_TILES - 1, 1)
                put_out(ROW_TILES - 2, 0)
                put_out(ROW_TILES - 1, 1)

            setup()
            for n in range(TILES):
                if n % ROW_TILES == 0:
                    dve.wait_ge(sem(f"x_loaded_{n // ROW_TILES}"), 16)
                own.did(v.bn_stats(stats[:, n, :], X[:, n, :]))
            split_weights()
            for s, stage in enumerate((ffn, recurrence, ffn, experts, heads, experts)[:STAGES]):
                stage(s)
            own.settle()
            dve.sem_inc(x_done, 1)


_NAMES = ['L0_attn_x', 'L0_attn_a_param', 'L0_attn_w_in', 'L0_attn_w_a', 'L0_ffn_proj', 'L0_ffn_C1', 'L0_ffn_Win1',
          'L0_ffn_Wout1', 'L0_ffn_C2', 'L0_ffn_Win2', 'L0_ffn_Wout2', 'L1_attn_in_proj_weight', 'L1_attn_in_proj_bias',
          'L1_attn_out_w', 'L1_attn_out_b', 'L1_ffn_sim_matrix', 'L1_ffn_gates', 'L1_ffn_q_proj', 'L1_ffn_k_proj',
          'L1_ffn_v_proj', 'L1_ffn_o_proj']


_SHAPES = {
    "early": {
        "ident": (0, P, P), "ones": (0, P, P), "causal": (0, P, P), "k_row": (0, P, E), "inv_k": (0, P, E), "seg": (0, P, TILES * E),
        "proj": (0, P, E), "c12": (0, 4 * E, 4 * R), "win1": (0, P, 2 * R), "b1": (0, P, 1), "b2": (0, P, 1),
        "wo2": (0, P, D), "a_param": (0, P, 1), "sim": (0, P, E), "gates": (0, P, E)},
    "split": {"wo1": (0, P, O), "win2": (0, P, OC * R), "pick": (0, 4 * E, E // 2 * P)},
    "late": {
        "wo": (0, P, E * HD), "w_qkv": (0, P, 3 * D), "b_qkv": (0, P, 3 * D), "w_out": (0, P, D), "b_out": (0, P, D), "fold": (0, P, P)},
}


def places():
    out, packed = {}, {}
    for pack, shapes in _SHAPES.items():
        at = 0
        for name, (lo, hi, n) in shapes.items():
            out[name] = (pack, lo, hi, at, n)
            at += n
        packed[pack] = at
    return out, packed


PLACES, PACKED = places()


def laid_out(i):
    k = np.arange(1, E + 1, dtype=np.float32)
    seg = np.ones((TILES, E), np.float32)
    seg[:, 0] = 0.0
    pick = np.zeros((2, 2, E, E // 2, 2, HD), np.float32)
    for e in range(E):
        pick[:, 0, e, e // 2, e % 2] = 1.0
    q, kk, v = (i[f"L1_ffn_{n}_proj"] for n in "qkv")
    c12 = np.zeros((2, 2, E, 4 * R), np.float32)
    c12[:, 0] = np.concatenate([i[f"L0_ffn_C{n}"] for n in (1, 1, 2, 2)], axis=1)
    c12 = c12.reshape(4 * E, 4 * R)
    parts = {
        "ident": np.eye(P, dtype=np.float32),
        "ones": np.ones((P, P), np.float32),
        "causal": np.triu(np.full((P, P), -1e30, np.float32), 1),
        "fold": np.tile(np.eye(HD, dtype=np.float32), (2, 2)),
        "k_row": np.broadcast_to(k, (P, E)),
        "inv_k": np.broadcast_to(1 / k, (P, E)),
        "seg": np.broadcast_to(seg.reshape(1, -1), (P, TILES * E)),
        "proj": i["L0_ffn_proj"],
        "c12": c12,
        "win1": np.tile(i["L0_ffn_Win1"][:D], (1, 2)),
        "b1": np.tile(i["L0_ffn_Win1"][D:].T, (2, 1)),
        "wo1": np.tile(i["L0_ffn_Wout1"].T, (2, 1)),
        "win2": i["L0_ffn_Win2"][:O].reshape(OC, P, R).transpose(1, 0, 2).reshape(P, OC * R),
        "b2": np.concatenate([i["L0_ffn_Win2"][O:].T, np.zeros((R, 1), np.float32)]),
        "wo2": np.tile(i["L0_ffn_Wout2"].T, (2, 1)),
        "a_param": i["L0_attn_a_param"].reshape(D, 1),
        "sim": i["L1_ffn_sim_matrix"],
        "gates": np.broadcast_to(i["L1_ffn_gates"], (P, E)),
        "pick": pick.reshape(4 * E, E // 2 * P),
        "wo": i["L1_ffn_o_proj"].reshape(E * HD // P, P, D).transpose(1, 0, 2).reshape(P, E * HD),
        "w_qkv": i["L1_attn_in_proj_weight"].T,
        "b_qkv": np.broadcast_to(i["L1_attn_in_proj_bias"], (P, 3 * D)),
        "w_out": i["L1_attn_out_w"].T,
        "b_out": np.broadcast_to(i["L1_attn_out_b"], (P, D)),
    }
    packs = {pack: np.zeros((P, n), np.float32) for pack, n in PACKED.items()}
    for name, (pack, lo, hi, at, n) in PLACES.items():
        packs[pack][lo:hi, at:at + n] = parts[name]
    return {
        **packs,
        "w_in": i["L0_attn_w_in"],
        "w_a": i["L0_attn_w_a"],
        "wqkv": np.concatenate([q, kk, v], axis=2).transpose(1, 0, 2).reshape(D, E * QKV),
    }


def kernel(**inputs):
    import concourse.bacc as bacc
    from concourse.bass_utils import run_bass_kernel_spmd

    nc = bacc.Bacc("TRN2", target_bir_lowering=False, num_devices=1)
    arrays = {"x_dram": np.ascontiguousarray(inputs["L0_attn_x"])}
    for name, a in laid_out({n: np.asarray(inputs[n]) for n in _NAMES}).items():
        arrays[f"{name}_dram"] = np.ascontiguousarray(a)
    aps = {n: nc.dram_tensor(n, a.shape, F32, kind="ExternalInput").ap() for n, a in arrays.items()}
    out = nc.dram_tensor("out_dram", (B, T, D), F32, kind="ExternalOutput").ap()
    program(nc, aps["x_dram"], out, {n[:-5]: ap for n, ap in aps.items() if n != "x_dram"})
    r = run_bass_kernel_spmd(nc, [arrays], core_ids=[0])
    return r.results[0]["out_dram"]
```
